# Optimizing a Trainium2 kernel written in Bass

```python
import numpy as np
import jax
import jax.numpy as jnp

def _softmax(x, axis=-1):
    return jax.nn.softmax(x, axis=axis)

def _gelu(x):
    return jax.nn.gelu(x, approximate=True)

def _silu(x):
    return jax.nn.silu(x)

def _sigmoid(x):
    return jax.nn.sigmoid(x)

def _layernorm(x, axis=-1, eps=1e-05):
    m = jnp.mean(x, axis=axis, keepdims=True)
    v = jnp.var(x, axis=axis, keepdims=True)
    return (x - m) / jnp.sqrt(v + eps)

def _scatter_add(tgt, idx, src, axis=0):
    return tgt.at[idx].add(src)

def _segment_sum(src, seg, n):
    return jax.ops.segment_sum(src, seg, n)
kernel_name = 'mk_vit_tower_cls_d1_tok_img768_r4_c898f3'

def setup_inputs(seed: int=0):
    np.random.seed(seed)
    _w = jnp.asarray

    def _rec_inputs():
        import jax
        import jax.numpy as jnp
        _rk = jax.random.key(seed)
        x = -0.000147625 + 0.999875 * jax.random.normal(jax.random.fold_in(_rk, 1), (64, 3, 224, 224), jnp.float32)
        cls_tok = 0.02 * jax.random.normal(jax.random.fold_in(_rk, 5), (1, 1, 192), jnp.float32)
        return (x, cls_tok)
    x, cls_tok = _rec_inputs()

    def _L0_tok_setup():
        import jax, jax.numpy as jnp
        import numpy as np
        PATCH = 16
        key = jax.random.key(seed)
        ks = jax.random.split(key, 5)
        B, C, H, W = (64, 3, 224, 224)
        D = 192
        NP = H // PATCH * (W // PATCH)
        return {'x': jax.random.normal(ks[0], (B, C, H, W), jnp.float32), 'conv_w': jax.random.normal(ks[1], (D, C, PATCH, PATCH), jnp.float32) * 0.02, 'conv_b': jax.random.normal(ks[2], (D,), jnp.float32) * 0.02, 'cls_token': jax.random.normal(ks[3], (1, 1, D), jnp.float32) * 0.02, 'pos_emb': jax.random.normal(ks[4], (1, NP + 1, D), jnp.float32) * 0.02}
    _L0_tok_all = _L0_tok_setup()
    _L0_tok_in = {k: v for k, v in _L0_tok_all.items() if k in ('conv_w', 'conv_b', 'cls_token', 'pos_emb')}
    del _L0_tok_all

    def _L0_attn_setup():
        import jax, jax.numpy as jnp
        import numpy as np
        B, L, D, H = (2, 512, 192, 12)
        HD = D // H
        ROPE_BASE = 10000.0

        def apply_rope(x):
            d = x.shape[-1]
            pos = jnp.arange(x.shape[2], dtype=jnp.float32)
            inv_freq = 1.0 / ROPE_BASE ** (jnp.arange(0, d, 2, dtype=jnp.float32) / d)
            ang = pos[:, None] * inv_freq[None, :]
            cos = jnp.concatenate([jnp.cos(ang), jnp.cos(ang)], axis=-1)
            sin = jnp.concatenate([jnp.sin(ang), jnp.sin(ang)], axis=-1)
            x1, x2 = jnp.split(x, 2, axis=-1)
            rot = jnp.concatenate([-x2, x1], axis=-1)
            return x * cos[None, None, :, :].astype(x.dtype) + rot * sin[None, None, :, :].astype(x.dtype)
        key = jax.random.key(seed)
        ks = jax.random.split(key, 9)
        s = 1.0 / np.sqrt(D)
        return {'query': jax.random.normal(ks[0], (B, L, D), dtype=jnp.float32), 'Wq': jax.random.uniform(ks[1], (D, D), jnp.float32, -s, s), 'bq': jax.random.uniform(ks[2], (D,), jnp.float32, -s, s), 'Wk': jax.random.uniform(ks[3], (D, D), jnp.float32, -s, s), 'bk': jax.random.uniform(ks[4], (D,), jnp.float32, -s, s), 'Wv': jax.random.uniform(ks[5], (D, D), jnp.float32, -s, s), 'bv': jax.random.uniform(ks[6], (D,), jnp.float32, -s, s), 'Wo': jax.random.uniform(ks[7], (D, D), jnp.float32, -s, s), 'bo': jax.random.uniform(ks[8], (D,), jnp.float32, -s, s)}
    _L0_attn_all = _L0_attn_setup()
    _L0_attn_in = {k: v for k, v in _L0_attn_all.items() if k in ('Wq', 'bq', 'Wk', 'bk', 'Wv', 'bv', 'Wo', 'bo')}
    del _L0_attn_all

    def _L0_ffn_setup():
        import jax, jax.numpy as jnp
        import numpy as np
        GT0 = [[0, 1, 0, 0, 1, 0], [0, 1, 0, 0, 0, 1], [0, 0, 1, 0, 1, 0], [0, 0, 1, 0, 0, 1], [0, 0, 0, 1, 1, 0], [0, 0, 0, 1, 0, 1]]
        NCLS = 6
        K = 1

        def _expert_pairs():
            pairs = []
            for i in range(NCLS):
                p = [(j - 1, k - 1) for j in range(1, 6) for k in range(1, 6) if j != k and GT0[i][j] == 1 and (GT0[i][k] == 1)]
                pairs.append(p)
            return pairs
        PAIRS = _expert_pairs()
        B, P, D, H = (64, 64, 192, 768)

        def _gelu(t):
            return jax.nn.gelu(t, approximate=False)
        key = jax.random.key(seed)
        ks = jax.random.split(key, 8)
        s = 0.02
        x = jax.random.normal(ks[0], (B, NCLS + P, D), dtype=jnp.float32)
        mids = jax.random.randint(ks[1], (B,), 0, 6)
        moe0_W1 = jax.random.normal(ks[2], (D, H), dtype=jnp.float32) * s
        moe0_b1 = jnp.zeros((H,), jnp.float32)
        moe0_W2 = jax.random.normal(ks[3], (H, D), dtype=jnp.float32) * s
        moe0_b2 = jnp.zeros((D,), jnp.float32)
        A1_W = jax.random.normal(ks[4], (5, D, H), dtype=jnp.float32) * s
        A1_b = jnp.zeros((5, H), jnp.float32)
        A2_W = jax.random.normal(ks[5], (5, H, D), dtype=jnp.float32) * s
        A2_b = jnp.zeros((5, D), jnp.float32)
        G_W = jax.random.normal(ks[6], (NCLS, D, 2), dtype=jnp.float32) * s
        return {'x': x, 'moe0_W1': moe0_W1, 'moe0_b1': moe0_b1, 'moe0_W2': moe0_W2, 'moe0_b2': moe0_b2, 'A1_W': A1_W, 'A1_b': A1_b, 'A2_W': A2_W, 'A2_b': A2_b, 'G_W': G_W, 'mids': mids}
    _L0_ffn_all = _L0_ffn_setup()
    _L0_ffn_in = {k: v for k, v in _L0_ffn_all.items() if k in ('moe0_W1', 'moe0_b1', 'moe0_W2', 'moe0_b2', 'A1_W', 'A1_b', 'A2_W', 'A2_b', 'G_W', 'mids')}
    del _L0_ffn_all
    return {'x': x, 'cls_tok': cls_tok, 'L0_tok_conv_w': _L0_tok_in['conv_w'], 'L0_tok_conv_b': _L0_tok_in['conv_b'], 'L0_tok_cls_token': _L0_tok_in['cls_token'], 'L0_tok_pos_emb': _L0_tok_in['pos_emb'], 'L0_attn_Wq': _L0_attn_in['Wq'], 'L0_attn_bq': _L0_attn_in['bq'], 'L0_attn_Wk': _L0_attn_in['Wk'], 'L0_attn_bk': _L0_attn_in['bk'], 'L0_attn_Wv': _L0_attn_in['Wv'], 'L0_attn_bv': _L0_attn_in['bv'], 'L0_attn_Wo': _L0_attn_in['Wo'], 'L0_attn_bo': _L0_attn_in['bo'], 'L0_ffn_moe0_W1': _L0_ffn_in['moe0_W1'], 'L0_ffn_moe0_b1': _L0_ffn_in['moe0_b1'], 'L0_ffn_moe0_W2': _L0_ffn_in['moe0_W2'], 'L0_ffn_moe0_b2': _L0_ffn_in['moe0_b2'], 'L0_ffn_A1_W': _L0_ffn_in['A1_W'], 'L0_ffn_A1_b': _L0_ffn_in['A1_b'], 'L0_ffn_A2_W': _L0_ffn_in['A2_W'], 'L0_ffn_A2_b': _L0_ffn_in['A2_b'], 'L0_ffn_G_W': _L0_ffn_in['G_W'], 'L0_ffn_mids': _L0_ffn_in['mids']}

def reference(x, cls_tok, L0_tok_conv_w, L0_tok_conv_b, L0_tok_cls_token, L0_tok_pos_emb, L0_attn_Wq, L0_attn_bq, L0_attn_Wk, L0_attn_bk, L0_attn_Wv, L0_attn_bv, L0_attn_Wo, L0_attn_bo, L0_ffn_moe0_W1, L0_ffn_moe0_b1, L0_ffn_moe0_W2, L0_ffn_moe0_b2, L0_ffn_A1_W, L0_ffn_A1_b, L0_ffn_A2_W, L0_ffn_A2_b, L0_ffn_G_W, L0_ffn_mids):
    import jax
    import jax.numpy as jnp

    def _L0_tok_ref(x, conv_w, conv_b, cls_token, pos_emb):
        import jax, jax.numpy as jnp
        import numpy as np
        PATCH = 16
        B, C, H, W = x.shape
        D = conv_w.shape[0]
        nh, nw = (H // PATCH, W // PATCH)
        patches = x.reshape(B, C, nh, PATCH, nw, PATCH).transpose(0, 2, 4, 1, 3, 5)
        patches = patches.reshape(B, nh * nw, C * PATCH * PATCH)
        w = conv_w.reshape(D, C * PATCH * PATCH)
        tokens = jnp.einsum('bnk,dk->bnd', patches, w) + conv_b
        cls = jnp.broadcast_to(cls_token, (B, 1, D))
        out = jnp.concatenate([cls, tokens], axis=1)
        return out + pos_emb

    def _L0_attn_ref(query, Wq, bq, Wk, bk, Wv, bv, Wo, bo):
        import jax, jax.numpy as jnp
        import numpy as np
        B, L, D, H = (2, 512, 192, 12)
        HD = D // H
        ROPE_BASE = 10000.0

        def apply_rope(x):
            d = x.shape[-1]
            pos = jnp.arange(x.shape[2], dtype=jnp.float32)
            inv_freq = 1.0 / ROPE_BASE ** (jnp.arange(0, d, 2, dtype=jnp.float32) / d)
            ang = pos[:, None] * inv_freq[None, :]
            cos = jnp.concatenate([jnp.cos(ang), jnp.cos(ang)], axis=-1)
            sin = jnp.concatenate([jnp.sin(ang), jnp.sin(ang)], axis=-1)
            x1, x2 = jnp.split(x, 2, axis=-1)
            rot = jnp.concatenate([-x2, x1], axis=-1)
            return x * cos[None, None, :, :].astype(x.dtype) + rot * sin[None, None, :, :].astype(x.dtype)
        b, l, _ = query.shape
        q = (query @ Wq.T + bq).reshape(b, l, H, HD).transpose(0, 2, 1, 3)
        k = (query @ Wk.T + bk).reshape(b, l, H, HD).transpose(0, 2, 1, 3)
        v = (query @ Wv.T + bv).reshape(b, l, H, HD).transpose(0, 2, 1, 3)
        q = apply_rope(q)
        k = apply_rope(k)
        scores = jnp.einsum('bhqd,bhkd->bhqk', q, k) / np.sqrt(HD).astype(np.float32)
        causal = jnp.triu(jnp.ones((l, l), dtype=bool), k=1)
        scores = jnp.where(causal[None, None, :, :], -jnp.inf, scores)
        attn = jax.nn.softmax(scores, axis=-1)
        out = jnp.einsum('bhqk,bhkd->bhqd', attn, v)
        out = out.transpose(0, 2, 1, 3).reshape(b, l, D)
        return out @ Wo.T + bo

    def _L0_ffn_ref(x, moe0_W1, moe0_b1, moe0_W2, moe0_b2, A1_W, A1_b, A2_W, A2_b, G_W, mids):
        import jax, jax.numpy as jnp
        import numpy as np
        GT0 = [[0, 1, 0, 0, 1, 0], [0, 1, 0, 0, 0, 1], [0, 0, 1, 0, 1, 0], [0, 0, 1, 0, 0, 1], [0, 0, 0, 1, 1, 0], [0, 0, 0, 1, 0, 1]]
        NCLS = 6
        K = 1

        def _expert_pairs():
            pairs = []
            for i in range(NCLS):
                p = [(j - 1, k - 1) for j in range(1, 6) for k in range(1, 6) if j != k and GT0[i][j] == 1 and (GT0[i][k] == 1)]
                pairs.append(p)
            return pairs
        PAIRS = _expert_pairs()
        B, P, D, H = (64, 64, 192, 768)

        def _gelu(t):
            return jax.nn.gelu(t, approximate=False)
        cls_tokens = x[:, :NCLS]
        patch_tokens = x[:, NCLS:]
        patch_out = _gelu(patch_tokens @ moe0_W1 + moe0_b1) @ moe0_W2 + moe0_b2
        cls_outs = []
        for i in range(NCLS):
            tok = cls_tokens[:, i]
            eouts = [_gelu(tok @ A1_W[a] + A1_b[a]) @ A2_W[c] + A2_b[c] for a, c in PAIRS[i]]
            out = jnp.stack(eouts, axis=-1)
            gate = jax.nn.softmax(tok @ G_W[i], axis=-1)
            thr = jnp.sort(gate, axis=-1)[..., -(K + 1)]
            mask = (gate > thr[..., None]).astype(gate.dtype)
            g = gate * mask
            g = g / jnp.clip(jnp.sum(g, axis=-1, keepdims=True), 1e-06)
            cls_outs.append(jnp.sum(out * g[:, None, :], axis=-1))
        cls_out = jnp.stack(cls_outs, axis=1)
        return jnp.concatenate([cls_out, patch_out], axis=1)
    h = _L0_tok_ref(x, L0_tok_conv_w, L0_tok_conv_b, L0_tok_cls_token, L0_tok_pos_emb)
    h = jnp.concatenate([jnp.broadcast_to(cls_tok, (h.shape[0], 1, h.shape[2])), h], axis=1)
    h = h + _L0_attn_ref(_layernorm(h, axis=-1), L0_attn_Wq, L0_attn_bq, L0_attn_Wk, L0_attn_bk, L0_attn_Wv, L0_attn_bv, L0_attn_Wo, L0_attn_bo)
    h = h + _L0_ffn_ref(_layernorm(h, axis=-1), L0_ffn_moe0_W1, L0_ffn_moe0_b1, L0_ffn_moe0_W2, L0_ffn_moe0_b2, L0_ffn_A1_W, L0_ffn_A1_b, L0_ffn_A2_W, L0_ffn_A2_b, L0_ffn_G_W, L0_ffn_mids)
    return h

_drawn_inputs = setup_inputs


def setup_inputs(seed=0):
    import zlib

    import numpy as np

    out = dict(_drawn_inputs(seed))
    spreads = {'L0_ffn_moe0_b1': (0.0, 0.1),
     'L0_ffn_moe0_b2': (0.0, 0.1),
     'L0_ffn_A1_b': (0.0, 0.8),
     'L0_ffn_A2_b': (0.0, 0.1)}
    factors = {'L0_attn_bq': 8.0, 'L0_attn_bk': 42.862}
    for name, (base, spread) in spreads.items():
        noise = np.random.default_rng([zlib.crc32(name.encode()), seed]).standard_normal(out[name].shape)
        drawn = base * np.exp(spread * noise) if base else spread * noise
        out[name] = jnp.asarray(drawn.astype(out[name].dtype))
    for name, factor in factors.items():
        out[name] = (out[name] * factor).astype(out[name].dtype)
    return out
```

```python
from contextlib import ExitStack

import numpy as np

import concourse.bass as bass
from concourse import mybir

F32 = mybir.dt.float32
F32R = mybir.dt.float32r
ALU = mybir.AluOpType
ACT = mybir.ActivationFunctionType

B = 64
D = 192
T = 198
T0, T1 = 128, T - 128
TILES = ((0, T0), (T0, T1))
KC = 6
H, HD = 12, 16
PAIRS = H // 2
HF = D // 2
FF = 768
FC = FF // 128
NCLS = 6
EPS = 1e-5
SCALE = HD ** -0.5
FAR = -1.0e30
STEPS = H + 3

GROUPS = ((0, 3), (0, 4), (1, 3), (1, 4), (2, 3), (2, 4))
COMBOS = [(i, e, (a, c) if e == 0 else (c, a)) for i, (a, c) in enumerate(GROUPS) for e in range(2)]


def phase_one(nc, h, ident, dram):
    with ExitStack() as ctx:
        def sb(name, shape, dt=F32):
            return ctx.enter_context(nc.sbuf_tensor(name, shape, dt))

        def sem(name):
            return ctx.enter_context(nc.semaphore(name))

        conv_w = sb("conv_w", [128, KC, D])
        embed = sb("embed", [128, 2, D])
        embed_pos = sb("embed_pos", [128, 2, D])
        wqkv = sb("wqkv", [HF + 1, 2, 3 * D])
        wo = sb("wo", [HF + 1, 2, D])
        cos = sb("cos", [128, 2, HD])
        sin = sb("sin", [128, 2, HD])
        mask0 = sb("mask0", [128, T0])
        mask1 = sb("mask1", [T1, T])
        x = sb("x", [128, KC, T])
        stats = sb("stats", [128, 2, 6])
        mv = sb("mv", [128, 2, 2])
        veps = sb("veps", [128, 2])
        minus_half = sb("minus_half", [128, 2])
        eps = sb("eps", [128, 2])
        carrier = sb("carrier", [1, 16])
        zeros = sb("zeros", [128, 2, D])
        rstd = sb("rstd", [128, 2])
        z = sb("z", [128, 2, D])
        zT = sb("zT", [HF + 1, 2, T])
        rope_c = sb("rope_c", [128, 2, 2 * D])
        rope_s = sb("rope_s", [128, 2, 2 * D])
        rope = sb("rope", [128, 2, 2 * D])
        parts = sb("parts", [128, 2, 2, H, 4, HD], F32R)
        partsT = sb("partsT", [128, PAIRS, 2, T], F32R)
        v_stage = sb("v_stage", [128, 2, D])
        v = sb("v", [128, 2, H, 32])
        masked = sb("masked", [128, 2, T0 + T])
        negmax = sb("negmax", [128, H, 2])
        probs = sb("probs", [128, 3, T0 + T])
        probsT = sb("probsT", [128, 2, T + T1])
        oT = sb("oT", [128, 3, T])
        rowsum_inv = sb("rowsum_inv", [128, 2, H])
        o = sb("o", [128, 2, D])
        onT = sb("onT", [HF + 1, 2, T])

        ps = [ctx.enter_context(nc.psum_tensor(f"ps{i}", [128, 512], F32)) for i in range(8)]
        ps_a, ps_b, ps_o0, ps_o1 = ps[0], ps[1], ps[2], ps[3]
        ps_s = ps[4:6]
        ps_p = ps[6:8]

        s_const = sem("s_const")
        s_preset = sem("s_preset")
        s_embed = sem("s_embed")
        s_x = sem("s_x")
        s_conv = sem("s_conv")
        s_h0 = sem("s_h0")
        s_stats = sem("s_stats")
        s_mv = sem("s_mv")
        s_veps = sem("s_veps")
        s_rstd = sem("s_rstd")
        s_z = sem("s_z")
        s_zT_ps = sem("s_zT_ps")
        s_zT = sem("s_zT")
        s_qk = sem("s_qk")
        s_qk_read = sem("s_qk_read")
        s_rope = sem("s_rope")
        s_hi = sem("s_hi")
        s_parts = sem("s_parts")
        s_v_ps = sem("s_v_ps")
        s_v_stage = sem("s_v_stage")
        s_v = sem("s_v")
        s_partsT_ps = sem("s_partsT_ps")
        s_partsT = sem("s_partsT")
        s_scores = sem("s_scores")
        s_masked = sem("s_masked")
        s_probs = sem("s_probs")
        s_pT_ps = sem("s_pT_ps")
        s_pT = sem("s_pT")
        s_pv = sem("s_pv")
        s_oT = sem("s_oT")
        s_o_ps = sem("s_o_ps")
        s_rsum = sem("s_rsum")
        s_o = sem("s_o")
        s_onT_ps = sem("s_onT_ps")
        s_onT = sem("s_onT")
        s_wo = sem("s_wo")
        s_h1 = sem("s_h1")

        consts = [(conv_w, dram["conv_w"]), (embed, dram["embed_a"]), (embed_pos, dram["embed_b"]),
                  (wqkv, dram["wqkv"]), (wo, dram["wo"]), (cos, dram["cos"]), (sin, dram["sin"]),
                  (mask0, dram["mask0"]), (mask1, dram["mask1"]), (ident, dram["ident"])]
        PRESETS = 19

        block = ctx.enter_context(nc.Block())

        @block.sync
        def _(sp):
            def load_x(m):
                if not (isinstance(m, int) and m == 0):
                    sp.wait_ge(s_conv, m * 2)
                sp.dma_start(x[:, :, :], dram["x"][bass.ds(m, 1)].rearrange("o p n -> p (o n)")
                             .rearrange("p (c t) -> p c t", c=KC)).then_inc(s_x, 16)

            load_x(0)
            for to, source in consts:
                sp.dma_start(to[:], source).then_inc(s_const, 16)
            with sp.Fori(1, B) as m:
                load_x(m)

        @block.gpsimd
        def _(pool):
            pool.memset(minus_half[:, :], -0.5).then_inc(s_preset, 1)
            pool.memset(eps[:, :], EPS).then_inc(s_preset, 1)
            pool.memset(mv[:, :, :], 1.0).then_inc(s_preset, 1)
            pool.memset(v[:, :, :, 0:HD], 0.0).then_inc(s_preset, 1)
            pool.memset(v[:, :, :, HD:HD + 1], 1.0).then_inc(s_preset, 1)
            pool.memset(v[:, :, :, HD + 1:32], 0.0).then_inc(s_preset, 1)
            pool.memset(v_stage[:, :, :], 0.0).then_inc(s_preset, 1)
            pool.memset(zeros[:, :, :], 0.0).then_inc(s_preset, 1)
            pool.wait_ge(s_preset, PRESETS)

            def rstd_of(m):
                if not (isinstance(m, int) and m == 0):
                    pool.wait_ge(s_z, m * 2)
                pool.wait_ge(s_mv, m * 2 + 2)
                pool.tensor_tensor(veps[:, :], mv[:, :, 1], eps[:, :], ALU.add).then_inc(s_veps, 1)
                pool.wait_ge(s_veps, m + 1)
                pool.tensor_tensor(rstd[:, :], veps[:, :], minus_half[:, :], ALU.pow).then_inc(s_rstd, 1)

            def twice(values, t, w):
                n = TILES[t][1]
                return values[0:n, t, w * D:(w + 1) * D].rearrange("p (h o d) -> p h o d", h=H, o=1)\
                    .broadcast_to([n, H, 2, HD])

            def split(m, t):
                n = TILES[t][1]
                pool.wait_ge(s_qk_read, m * 2 + t + 1)
                if not (isinstance(m, int) and m == 0):
                    pool.wait_ge(s_partsT_ps, m * PAIRS)
                pool.tensor_tensor(rope[0:n, t, :], rope_c[0:n, t, :], rope_s[0:n, t, :], ALU.add)\
                    .then_inc(s_rope, 1)
                for w in range(2):
                    hi = parts[0:n, t, w, :, 0:2, :] if w == 0 else parts[0:n, t, w, :, 0:4:2, :]
                    pool.tensor_tensor(hi, twice(rope_c, t, w), twice(rope_s, t, w), ALU.add).then_inc(s_hi, 1)
                pool.wait_ge(s_rope, m * 2 + t + 1)
                pool.wait_ge(s_hi, m * 4 + 2 * t + 2)
                for w in range(2):
                    hi = parts[0:n, t, w, :, 0:2, :] if w == 0 else parts[0:n, t, w, :, 0:4:2, :]
                    lo = parts[0:n, t, w, :, 2:4, :] if w == 0 else parts[0:n, t, w, :, 1:4:2, :]
                    pool.tensor_tensor(lo, twice(rope, t, w), hi.bitcast(F32), ALU.subtract).then_inc(s_parts, 1)

            def spread_v(m):
                if not (isinstance(m, int) and m == 0):
                    pool.wait_ge(s_pv, m * H)
                pool.wait_ge(s_v_stage, m * 2 + 2)
                pool.tensor_tensor(v[:, :, :, 0:HD], v_stage[:, :, :].rearrange("p t (h d) -> p t h d", h=H),
                                   zeros[:, :, :].rearrange("p t (h d) -> p t h d", h=H), ALU.add).then_inc(s_v, 1)

            def image(m):
                rstd_of(m)
                split(m, 0)
                split(m, 1)
                spread_v(m)

            image(0)
            with pool.Fori(1, B) as m:
                image(m)

        @block.tensor
        def _(pe):
            def conv(m, t, first):
                at, n = TILES[t]
                if t == 0:
                    pe.wait_ge(s_x, m * 16 + 16)
                    if not first:
                        pe.wait_ge(s_partsT, m * PAIRS)
                for c in range(KC):
                    mm = pe.matmul(ps_a[0:n, t * D:(t + 1) * D], x[:, c, at:at + n], conv_w[:, c, :],
                                   start=(c == 0), stop=(c == KC - 1))
                mm.then_inc(s_conv, 1)

            def z_transpose(m, after_back):
                pe.wait_ge(s_z, m * 2 + 2)
                if after_back is not None:
                    pe.wait_ge(s_o, after_back * 2 + 1)
                for t, (at, n) in enumerate(TILES):
                    for k in range(2):
                        mm = pe.transpose(ps_b[0:HF, k * T + at:k * T + at + n],
                                          z[0:n, t, k * HF:(k + 1) * HF], ident[0:n, 0:n])
                mm.then_inc(s_zT_ps, 1)

            def project(to, m, t, first, last):
                at, n = TILES[t]
                pe.matmul(to, zT[0:HF + 1, 0, at:at + n], wqkv[:, 0, first:last], start=True, stop=False)
                return pe.matmul(to, zT[0:HF, 1, at:at + n], wqkv[0:HF, 1, first:last], start=False, stop=True)

            def qk(m, t):
                n = TILES[t][1]
                if t == 0:
                    pe.wait_ge(s_zT, m + 1)
                else:
                    pe.wait_ge(s_qk_read, m * 2 + 1)
                project(ps_b[0:n, 0:2 * D], m, t, 0, 2 * D).then_inc(s_qk, 1)

            def values(m, after_back):
                if after_back is not None:
                    pe.wait_ge(s_h1, after_back * 2 + 2)
                else:
                    pe.wait_ge(s_h0, m * 2 + 2)
                for t, (at, n) in enumerate(TILES):
                    mm = project(ps_a[0:n, t * D:(t + 1) * D], m, t, 2 * D, 3 * D)
                mm.then_inc(s_v_ps, 1)

            def parts_transpose(m, p):
                bank = ps_a if p % 2 else ps_b
                if p == 0:
                    pe.wait_ge(s_parts, m * 4 + 4)
                elif p == 1:
                    pe.wait_ge(s_v_stage, m * 2 + 2)
                else:
                    pe.wait_ge(s_partsT, m * PAIRS + p - 1)
                for w in range(2):
                    for t, (at, n) in enumerate(TILES):
                        pair = parts[0:n, t, w, 2 * p:2 * p + 2, :, :].rearrange("p h b d -> p (h b d)")
                        mm = pe.transpose(bank[:, w * T + at:w * T + at + n], pair.bitcast(F32), ident[0:n, 0:n])
                mm.then_inc(s_partsT_ps, 1)

            def scores(i, k, first):
                p, r = k // 2, 64 * (k % 2)
                if k % 2 == 0:
                    pe.wait_ge(s_partsT, i * PAIRS + p + 1)
                if not (first and k < 2):
                    pe.wait_ge(s_masked, i * H + k - 1)
                q, kk = partsT[r:r + 64, p, 0, :], partsT[r:r + 64, p, 1, :]
                bank = ps_s[k % 2]
                pe.matmul(bank[0:T0, 0:T0], q[:, 0:T0], kk[:, 0:T0], start=True, stop=True)
                pe.matmul(bank[0:T1, T0:T0 + T], q[:, T0:T], kk[:, 0:T], start=True, stop=True)\
                    .then_inc(s_scores, 1)

            def probs_transpose(i, k, first):
                pe.wait_ge(s_probs, i * H + k + 1)
                if not (first and k < 2):
                    pe.wait_ge(s_pT, i * H + k - 1)
                bank, p = ps_p[k % 2], probs[:, k % 3, :]
                pe.transpose(bank[0:T0, 0:T0], p[0:T0, 0:T0], ident[:, :])
                pe.transpose(bank[0:T0, T0:T], p[0:T1, T0:2 * T0], ident[0:T1, 0:T1])
                pe.transpose(bank[0:T1, T:T + T1], p[0:T1, 2 * T0:T0 + T], ident[0:T1, 0:T1])\
                    .then_inc(s_pT_ps, 1)

            def pv(i, k, first):
                pe.wait_ge(s_pT, i * H + k + 1)
                if k == 0:
                    pe.wait_ge(s_v, i + 1)
                if k == 0 and not first:
                    pe.wait_ge(s_oT, i * 2 - 1)
                if k == 8 and not first:
                    pe.wait_ge(s_oT, i * 2)
                g, r = k // 4, 32 * (k % 4)
                bank, at = (ps_o0, g * T) if g < 2 else (ps_o1, 0)
                pT = probsT[:, k % 2, :]
                pe.matmul(bank[r:r + 32, at:at + T], v[:, 0, k, :], pT[:, 0:T], start=True, stop=False,
                          tile_position=(0, r))
                pe.matmul(bank[r:r + 32, at + T0:at + T], v[0:T1, 1, k, :], pT[0:T1, T:T + T1],
                          start=False, stop=True, tile_position=(0, r)).then_inc(s_pv, 1)

            def o_transpose(b, t, front, last=False):
                at, n = TILES[t]
                if t == 0:
                    pe.wait_ge(s_oT, b * 2 + 2)
                if t == 1 and front:
                    pe.wait_ge(s_h0, b * 2 + 6)
                if t == 0 and last:
                    pe.wait_ge(s_h1, b * 2)
                if t == 0 and not last:
                    pe.wait_ge(s_partsT, b * PAIRS + 2 * PAIRS)
                bank = ps_a if t else ps_b
                for g in range(3):
                    mm = pe.transpose(bank[0:n, g * 128:(g + 1) * 128], oT[:, g, at:at + n], ident[:, :])
                mm.then_inc(s_o_ps, 1)

            def on_transpose(b):
                pe.wait_ge(s_o, b * 2 + 2)
                for t, (at, n) in enumerate(TILES):
                    for k in range(2):
                        mm = pe.transpose(ps_a[0:HF, k * T + at:k * T + at + n],
                                          o[0:n, t, k * HF:(k + 1) * HF], ident[0:n, 0:n])
                mm.then_inc(s_onT_ps, 1)

            def out_project(b):
                pe.wait_ge(s_onT, b + 1)
                for t, (at, n) in enumerate(TILES):
                    to = ps_a[0:n, t * D:(t + 1) * D]
                    pe.matmul(to, onT[:, 0, at:at + n], wo[:, 0, :], start=True, stop=False)
                    mm = pe.matmul(to, onT[0:HF, 1, at:at + n], wo[0:HF, 1, :], start=False, stop=True)
                mm.then_inc(s_wo, 1)

            def step(i, k, first=False, front=True, back=True):
                if k < H:
                    scores(i, k, first)
                if 2 <= k < H + 2:
                    probs_transpose(i, k - 2, first)
                if k >= 3:
                    pv(i, k - 3, first)
                if front and k < 2:
                    conv(i + 1, k, False)
                if back and k == 2:
                    o_transpose(i - 1, 0, front)
                if back and k == 3:
                    o_transpose(i - 1, 1, front)
                if front and k == 5:
                    z_transpose(i + 1, i - 1 if back else None)
                if back and k == 6:
                    on_transpose(i - 1)
                if front and k in (7, 9):
                    qk(i + 1, (k - 7) // 2)
                if back and k == 8:
                    out_project(i - 1)
                if front and k == 10:
                    values(i + 1, i - 1 if back else None)
                if front and k >= 12:
                    parts_transpose(i + 1, 2 * (k - 12))
                    parts_transpose(i + 1, 2 * (k - 12) + 1)

            pe.wait_ge(s_const, 16 * len(consts))
            pe.wait_ge(s_preset, PRESETS)
            conv(0, 0, True)
            conv(0, 1, True)
            z_transpose(0, None)
            qk(0, 0)
            qk(0, 1)
            values(0, None)
            for p in range(PAIRS):
                parts_transpose(0, p)
            for k in range(STEPS):
                step(0, k, first=True, back=False)
            with pe.Fori(1, B - 1) as i:
                for k in range(STEPS):
                    step(i, k)
            for k in range(STEPS):
                step(B - 1, k, front=False)
            o_transpose(B - 1, 0, False, last=True)
            o_transpose(B - 1, 1, False, last=True)
            on_transpose(B - 1)
            out_project(B - 1)

        @block.scalar
        def _(act):
            act.wait_ge(s_preset, PRESETS)

            def exps(i, k, first):
                act.wait_ge(s_masked, i * H + k + 1)
                if not (first and k < 3):
                    act.wait_ge(s_pT_ps, i * H + k - 2)
                act.activation(probs[0:T0, k % 3, 0:T0], masked[0:T0, k % 2, 0:T0], ACT.Exp,
                               bias=negmax[0:T0, k, 0:1], scale=-1.0)
                act.activation(probs[0:T1, k % 3, T0:T0 + T], masked[0:T1, k % 2, T0:T0 + T], ACT.Exp,
                               bias=negmax[0:T1, k, 1:2], scale=-1.0).then_inc(s_probs, 1)

            def z_copy(m, first):
                act.wait_ge(s_zT_ps, m + 1)
                if not first:
                    act.wait_ge(s_v_ps, m)
                act.activation(zT[0:HF, :, :], ps_b[0:HF, 0:2 * T].rearrange("p (k t) -> p k t", k=2), ACT.Copy)\
                    .then_inc(s_zT, 1)

            def on_copy(b, first):
                act.wait_ge(s_onT_ps, b + 1)
                if not first:
                    act.wait_ge(s_wo, b)
                act.activation(onT[0:HF, :, :], ps_a[0:HF, 0:2 * T].rearrange("p (k t) -> p k t", k=2), ACT.Copy)\
                    .then_inc(s_onT, 1)

            def v_copy(m, first):
                act.wait_ge(s_v_ps, m + 1)
                if not first:
                    act.wait_ge(s_v, m)
                for t, (at, n) in enumerate(TILES):
                    act.activation(v_stage[0:n, t, :], ps_a[0:n, t * D:(t + 1) * D], ACT.Copy)\
                        .then_inc(s_v_stage, 1)

            def parts_copy(m, p, first):
                act.wait_ge(s_partsT_ps, m * PAIRS + p + 1)
                if not first:
                    act.wait_ge(s_scores, m * H - H + 2 * p + 2)
                bank = ps_a if p % 2 else ps_b
                act.activation(partsT[:, p, :, :], bank[:, 0:2 * T].rearrange("p (w t) -> p w t", w=2), ACT.Copy)\
                    .then_inc(s_partsT, 1)

            def o_copy(i, half, first):
                act.wait_ge(s_pv, i * H + (8 if half == 0 else 12))
                if not first and half == 0:
                    act.wait_ge(s_o_ps, i * 2)
                if half == 0:
                    act.activation(oT[:, 0:2, :], ps_o0[:, 0:2 * T].rearrange("p (g t) -> p g t", g=2), ACT.Copy)\
                        .then_inc(s_oT, 1)
                else:
                    act.activation(oT[:, 2, :], ps_o1[:, 0:T], ACT.Copy).then_inc(s_oT, 1)

            def step(i, k, first=False, front=True, back=True, first_back=False):
                if k < H:
                    exps(i, k, first)
                if front and k == 5:
                    z_copy(i + 1, False)
                if back and k == 6:
                    on_copy(i - 1, first_back)
                if front and k == 10:
                    v_copy(i + 1, False)
                if k == 11:
                    o_copy(i, 0, first)
                if front and k >= 12:
                    parts_copy(i + 1, 2 * (k - 12), False)
                    parts_copy(i + 1, 2 * (k - 12) + 1, False)
                if k == 14:
                    o_copy(i, 1, first)

            z_copy(0, True)
            v_copy(0, True)
            for p in range(PAIRS):
                parts_copy(0, p, True)
            for k in range(STEPS):
                step(0, k, first=True, back=False)
            for k in range(STEPS):
                step(1, k, first_back=True)
            with act.Fori(2, B - 1) as i:
                for k in range(STEPS):
                    step(i, k)
            for k in range(STEPS):
                step(B - 1, k, front=False)
            on_copy(B - 1, False)

        @block.vector
        def _(dve):
            dve.memset(zT[HF:HF + 1, :, :], 1.0).then_inc(s_preset, 1)
            dve.memset(onT[HF:HF + 1, :, :], 1.0).then_inc(s_preset, 1)
            for bank in ps:
                dve.memset(bank[:, :], 0.0).then_inc(s_preset, 1)
            dve.wait_ge(s_const, 16 * len(consts))
            dve.tensor_tensor(embed[:, :, :], embed[:, :, :], embed_pos[:, :, :], ALU.add).then_inc(s_preset, 1)
            dve.wait_ge(s_preset, PRESETS)

            def row_max(i, k, first):
                if not (first and k < 2):
                    dve.wait_ge(s_probs, i * H + k - 1)
                dve.wait_ge(s_scores, i * H + k + 1)
                dve.memset(carrier[:, k:k + 1], 0.0)
                bank = ps_s[k % 2]
                dve.tensor_tensor_reduce(masked[0:T0, k % 2, 0:T0], bank[0:T0, 0:T0], mask0[:, :], -SCALE, 1e38,
                                         ALU.add, ALU.min, negmax[0:T0, k, 0:1])
                dve.tensor_tensor_reduce(masked[0:T1, k % 2, T0:T0 + T], bank[0:T1, T0:T0 + T], mask1[:, :], -SCALE,
                                         1e38, ALU.add, ALU.min, negmax[0:T1, k, 1:2]).then_inc(s_masked, 1)

            def probs_copy(i, k, first):
                dve.wait_ge(s_pT_ps, i * H + k + 1)
                if not (first and k < 2):
                    dve.wait_ge(s_pv, i * H + k - 1)
                dve.tensor_copy(probsT[:, k % 2, 0:T], ps_p[k % 2][:, 0:T])
                dve.tensor_copy(probsT[0:T1, k % 2, T:T + T1], ps_p[k % 2][0:T1, T:T + T1]).then_inc(s_pT, 1)

            def h_tile(m, t, n):
                return h[0:n, bass.ds(m, 1), t, :].rearrange("p o d -> p (o d)")

            def embed_add(m, t):
                n = TILES[t][1]
                dve.wait_ge(s_conv, m * 2 + 2)
                dve.tensor_tensor(h_tile(m, t, n), ps_a[0:n, t * D:(t + 1) * D], embed[0:n, t, :], ALU.add)\
                    .then_inc(s_h0, 1)

            def moments(m, first):
                dve.wait_ge(s_h0, m * 2 + 2)
                dve.memset(carrier[:, 12:13], 0.0)
                for t, (at, n) in enumerate(TILES):
                    dve.bn_stats(stats[0:n, t, :], h_tile(m, t, n)).then_inc(s_stats, 1)
                if not first:
                    dve.wait_ge(s_rstd, m)
                dve.wait_ge(s_stats, m * 2 + 2)
                dve.memset(carrier[:, 13:14], 0.0)
                for t, (at, n) in enumerate(TILES):
                    dve.bn_aggr(mv[0:n, t, :], stats[0:n, t, :]).then_inc(s_mv, 1)

            def normalise(m, first):
                dve.wait_ge(s_rstd, m + 1)
                if not first:
                    dve.wait_ge(s_zT_ps, m)
                for t, (at, n) in enumerate(TILES):
                    dve.tensor_scalar(z[0:n, t, :], h_tile(m, t, n), mv[0:n, t, 0:1], rstd[0:n, t:t + 1],
                                      ALU.subtract, ALU.mult).then_inc(s_z, 1)

            def rotate(m, t, first):
                n = TILES[t][1]
                dve.wait_ge(s_qk, m * 2 + t + 1)
                if not first:
                    dve.wait_ge(s_hi, m * 4 + 2 * t - 2)
                heads = ps_b[0:n, 0:2 * D].rearrange("p (h d) -> p h d", d=HD)
                to_c = rope_c[0:n, t, :].rearrange("p (h d) -> p h d", d=HD)
                to_s = rope_s[0:n, t, :].rearrange("p (h d) -> p h d", d=HD)
                half = HD // 2

                def table(which, a, b):
                    return which[0:n, t, a:b].rearrange("p (o d) -> p o d", o=1).broadcast_to([n, 2 * H, b - a])

                dve.tensor_tensor(to_c, heads, table(cos, 0, HD), ALU.mult)
                dve.tensor_tensor(to_s[:, :, 0:half], heads[:, :, half:HD], table(sin, 0, half), ALU.mult)
                dve.tensor_tensor(to_s[:, :, half:HD], heads[:, :, 0:half], table(sin, half, HD), ALU.mult)\
                    .then_inc(s_qk_read, 1)

            def o_normalise(b, t, first):
                n = TILES[t][1]
                dve.wait_ge(s_o_ps, b * 2 + t + 1)
                heads = (ps_a if t else ps_b)[0:n, 0:3 * 128].rearrange("p (h d) -> p h d", d=32)
                dve.reciprocal(rowsum_inv[0:n, t, :], heads[:, :, HD]).then_inc(s_rsum, 1)
                dve.wait_ge(s_rsum, b * 2 + t + 1)
                if not first:
                    dve.wait_ge(s_onT_ps, b)
                dve.tensor_tensor(o[0:n, t, :].rearrange("p (h d) -> p h d", d=HD), heads[:, :, 0:HD],
                                  rowsum_inv[0:n, t, :].rearrange("p (h o) -> p h o", o=1)
                                  .broadcast_to([n, H, HD]), ALU.mult).then_inc(s_o, 1)

            def residual(b):
                dve.wait_ge(s_wo, b + 1)
                for t, (at, n) in enumerate(TILES):
                    dve.tensor_tensor(h_tile(b, t, n), h_tile(b, t, n), ps_a[0:n, t * D:(t + 1) * D], ALU.add)\
                        .then_inc(s_h1, 1)

            def step(i, k, first=False, front=True, back=True, first_back=False):
                if k < H:
                    row_max(i, k, first)
                if 2 <= k < H + 2:
                    probs_copy(i, k - 2, first)
                if front and k == 2:
                    embed_add(i + 1, 0)
                    embed_add(i + 1, 1)
                    moments(i + 1, False)
                if back and k in (3, 4):
                    o_normalise(i - 1, k - 3, first_back)
                if front and k == 4:
                    normalise(i + 1, False)
                if front and k in (7, 9):
                    rotate(i + 1, (k - 7) // 2, False)
                if back and k == 8:
                    residual(i - 1)

            embed_add(0, 0)
            embed_add(0, 1)
            moments(0, True)
            normalise(0, True)
            rotate(0, 0, True)
            rotate(0, 1, True)
            for k in range(STEPS):
                step(0, k, first=True, back=False)
            for k in range(STEPS):
                step(1, k, first_back=True)
            with dve.Fori(2, B - 1) as i:
                for k in range(STEPS):
                    step(i, k)
            for k in range(STEPS):
                step(B - 1, k, front=False)
            o_normalise(B - 1, 0, False)
            o_normalise(B - 1, 1, False)
            residual(B - 1)


def phase_two(nc, h, ident, dram, out, a1, a2, s_experts):
    with ExitStack() as ctx:
        def sb(name, shape, dt=F32):
            return ctx.enter_context(nc.sbuf_tensor(name, shape, dt))

        def sem(name):
            return ctx.enter_context(nc.semaphore(name))

        w1 = sb("w1", [HF + 1, 2, FF])
        w2 = sb("w2", [128, FC, D])
        b2 = sb("b2", [128, D])
        stats = sb("f_stats", [128, 2, 6])
        mv = sb("f_mv", [128, 2, 2])
        veps = sb("f_veps", [128, 2])
        minus_half = sb("f_minus_half", [128, 2])
        eps = sb("f_eps", [128, 2])
        carrier = sb("f_carrier", [1, 2])
        rstd = sb("f_rstd", [128, 2])
        z = sb("f_z", [128, 2, D])
        zT = sb("f_zT", [HF + 1, 2, T])
        hidden = sb("hidden", [128, FC, T])
        h_b2 = sb("h_b2", [128, 2, D])
        result = sb("result", [128, 2, D])

        ps = [ctx.enter_context(nc.psum_tensor(f"f_ps{i}", [128, 512], F32)) for i in range(6)]
        ps_up, ps_z, ps_down = ps[0:3], ps[3], ps[4:6]

        s_w = sem("f_w")
        s_preset = sem("f_preset")
        s_stats = sem("f_stats_done")
        s_mv = sem("f_mv_done")
        s_veps = sem("f_veps_done")
        s_rstd = sem("f_rstd_done")
        s_z = sem("f_z_done")
        s_zT_ps = sem("f_zT_ps")
        s_zT = sem("f_zT_done")
        s_up = sem("f_up")
        s_gelu = sem("f_gelu")
        s_down = sem("f_down")
        s_hb = sem("f_hb")
        s_result = sem("f_result")
        s_stored = sem("f_stored")

        loads = [(w1, dram["w1"]), (w2, dram["w2"]), (b2, dram["b2"])]
        PRESETS = 4
        block = ctx.enter_context(nc.Block())

        @block.sync
        def _(sp):
            for to, source in loads:
                sp.dma_start(to[:], source).then_inc(s_w, 16)
            sp.dma_start(a1[:], dram["a1"]).then_inc(s_experts, 16)
            sp.dma_start(a2[:], dram["a2"]).then_inc(s_experts, 16)
            with sp.Fori(0, B) as j:
                sp.wait_ge(s_result, j * 2 + 1)
                sp.dma_start(out[bass.ds(j, 1), NCLS:T0, :].rearrange("o p d -> p (o d)"), result[NCLS:T0, 0, :])\
                    .then_inc(s_stored, 16)
                sp.wait_ge(s_result, j * 2 + 2)
                sp.dma_start(out[bass.ds(j, 1), T0:T, :].rearrange("o p d -> p (o d)"), result[0:T1, 1, :])\
                    .then_inc(s_stored, 16)
            sp.wait_ge(s_stored, 32 * B)

        def h_tile(m, t, n):
            return h[0:n, bass.ds(m, 1), t, :].rearrange("p o d -> p (o d)")

        @block.gpsimd
        def _(pool):
            pool.memset(minus_half[:, :], -0.5).then_inc(s_preset, 1)
            pool.memset(eps[:, :], EPS).then_inc(s_preset, 1)
            pool.memset(mv[:, :, :], 1.0).then_inc(s_preset, 1)
            pool.wait_ge(s_preset, PRESETS)
            pool.wait_ge(s_w, 16 * len(loads))

            def image(j, first):
                if not first:
                    pool.wait_ge(s_z, j * 2)
                pool.wait_ge(s_mv, j * 2 + 2)
                pool.tensor_tensor(veps[:, :], mv[:, :, 1], eps[:, :], ALU.add).then_inc(s_veps, 1)
                pool.wait_ge(s_veps, j + 1)
                pool.tensor_tensor(rstd[:, :], veps[:, :], minus_half[:, :], ALU.pow).then_inc(s_rstd, 1)
                if not first:
                    pool.wait_ge(s_result, j * 2)
                for t, (at, n) in enumerate(TILES):
                    pool.tensor_tensor(h_b2[0:n, t, :], h_tile(j, t, n), b2[0:n, :], ALU.add).then_inc(s_hb, 1)

            image(0, True)
            with pool.Fori(1, B) as j:
                image(j, False)

        @block.tensor
        def _(pe):
            pe.wait_ge(s_preset, PRESETS)
            pe.wait_ge(s_w, 16 * len(loads))

            def transpose_z(j):
                pe.wait_ge(s_z, j * 2 + 2)
                for t, (at, n) in enumerate(TILES):
                    for k in range(2):
                        mm = pe.transpose(ps_z[0:HF, k * T + at:k * T + at + n],
                                          z[0:n, t, k * HF:(k + 1) * HF], ident[0:n, 0:n])
                mm.then_inc(s_zT_ps, 1)

            def up(j, first):
                pe.wait_ge(s_zT, j + 1)
                for u in range(FC // 2):
                    if not first:
                        pe.wait_ge(s_gelu, j * 3 - 2 + u)
                    for c in (2 * u, 2 * u + 1):
                        to = ps_up[u][:, (c % 2) * T:(c % 2 + 1) * T]
                        pe.matmul(to, w1[:, 0, c * 128:(c + 1) * 128], zT[:, 0, :], start=True, stop=False)
                        mm = pe.matmul(to, w1[0:HF, 1, c * 128:(c + 1) * 128], zT[0:HF, 1, :],
                                       start=False, stop=True)
                    mm.then_inc(s_up, 1)

            def down(j, first):
                for t, (at, n) in enumerate(TILES):
                    if not first:
                        pe.wait_ge(s_result, j * 2 - 1 + t)
                    for c in range(FC):
                        if t == 0 and c % 2 == 0:
                            pe.wait_ge(s_gelu, j * 3 + c // 2 + 1)
                        mm = pe.matmul(ps_down[t][0:n, 0:D], hidden[:, c, at:at + n], w2[:, c, :],
                                       start=(c == 0), stop=(c == FC - 1))
                    mm.then_inc(s_down, 1)

            def image(j, first=False, last=False):
                up(j, first)
                if not last:
                    transpose_z(j + 1)
                down(j, first)

            transpose_z(0)
            image(0, first=True)
            with pe.Fori(1, B - 1) as j:
                image(j)
            image(B - 1, last=True)

        @block.scalar
        def _(act):
            act.wait_ge(s_preset, PRESETS)

            def z_copy(j, first):
                act.wait_ge(s_zT_ps, j + 1)
                if not first:
                    act.wait_ge(s_up, j * 3)
                act.activation(zT[0:HF, :, :], ps_z[0:HF, 0:2 * T].rearrange("p (k t) -> p k t", k=2), ACT.Copy)\
                    .then_inc(s_zT, 1)

            def gelus(j, first):
                for u in range(FC // 2):
                    act.wait_ge(s_up, j * 3 + u + 1)
                    if not first:
                        act.wait_ge(s_down, j * 2)
                    act.activation(hidden[:, 2 * u:2 * u + 2, :],
                                   ps_up[u][:, 0:2 * T].rearrange("p (c t) -> p c t", c=2), ACT.Gelu)\
                        .then_inc(s_gelu, 1)

            z_copy(0, True)
            gelus(0, True)
            z_copy(1, False)
            with act.Fori(1, B - 1) as j:
                gelus(j, False)
                z_copy(j + 1, False)
            gelus(B - 1, False)

        @block.vector
        def _(dve):
            dve.memset(zT[HF:HF + 1, :, :], 1.0).then_inc(s_preset, 1)
            dve.wait_ge(s_preset, PRESETS)

            def normalise(j, first):
                for t, (at, n) in enumerate(TILES):
                    dve.bn_stats(stats[0:n, t, :], h_tile(j, t, n)).then_inc(s_stats, 1)
                if not first:
                    dve.wait_ge(s_rstd, j)
                dve.wait_ge(s_stats, j * 2 + 2)
                dve.memset(carrier[:, 0:1], 0.0)
                for t, (at, n) in enumerate(TILES):
                    dve.bn_aggr(mv[0:n, t, :], stats[0:n, t, :]).then_inc(s_mv, 1)
                dve.wait_ge(s_rstd, j + 1)
                if not first:
                    dve.wait_ge(s_zT_ps, j)
                for t, (at, n) in enumerate(TILES):
                    dve.tensor_scalar(z[0:n, t, :], h_tile(j, t, n), mv[0:n, t, 0:1], rstd[0:n, t:t + 1],
                                      ALU.subtract, ALU.mult).then_inc(s_z, 1)

            def finish(j, first):
                for t, (at, n) in enumerate(TILES):
                    dve.wait_ge(s_down, j * 2 + t + 1)
                    dve.wait_ge(s_hb, j * 2 + t + 1)
                    if not first:
                        dve.wait_ge(s_stored, j * 32)
                    dve.tensor_tensor(result[0:n, t, :], ps_down[t][0:n, 0:D], h_b2[0:n, t, :], ALU.add)\
                        .then_inc(s_result, 1)

            normalise(0, True)
            normalise(1, False)
            finish(0, True)
            with dve.Fori(1, B - 1) as j:
                normalise(j + 1, False)
                finish(j, False)
            finish(B - 1, False)


def phase_three(nc, h, ident, dram, out, a1, a2, s_experts):
    NT = NCLS // 2
    WIDE = [128] * NT + [64 * NT] * 2

    with ExitStack() as ctx:
        def sb(name, shape, dt=F32):
            return ctx.enter_context(nc.sbuf_tensor(name, shape, dt))

        def sem(name):
            return ctx.enter_context(nc.semaphore(name))

        gate_w = sb("gate_w", [HF, 2, 2 * NCLS])
        b2 = sb("e_b2", [128, NT, 2, D])
        hc = sb("hc", [128, NT, D])
        stats = sb("e_stats", [128, NT, 6])
        mv = sb("e_mv", [128, NT, 2])
        veps = sb("e_veps", [128, NT])
        minus_half = sb("e_minus_half", [128, NT])
        rstd = sb("e_rstd", [128, NT])
        z = sb("e_z", [128, NT, D])
        zT = sb("e_zT", [HF + 1, 2, NT * 128])
        hidden = sb("e_hidden", [128, FC, 2 * NT * 128])
        logits = sb("logits", [128, NT, 2])
        top = sb("top", [128, NT])
        shifted = sb("shifted", [128, NT, 2])
        expd = sb("expd", [128, NT, 2])
        total = sb("total", [128, NT])
        total_inv = sb("total_inv", [128, NT])
        gate = sb("gate", [128, NT, 2])
        least = sb("least", [128, NT])
        above = sb("above", [128, NT, 2])
        kept = sb("kept", [128, NT, 2])
        kept_sum = sb("kept_sum", [128, NT])
        kept_clip = sb("kept_clip", [128, NT])
        kept_inv = sb("kept_inv", [128, NT])
        share = sb("share", [128, NT, 2])
        y = sb("e_y", [128, NT, 2, D])
        mix = sb("e_mix", [128, NT, D])
        res = sb("e_res", [128, NT, D])

        ps = [ctx.enter_context(nc.psum_tensor(f"e_ps{i}", [128, 512], F32)) for i in range(8)]
        ps_z, ps_gate, ps_up, ps_y = ps[0:2], ps[2], ps[3:5], ps[5:8]

        s_in = sem("e_in")
        s_preset = sem("e_preset")
        s_stats = sem("e_stats_done")
        s_mv = sem("e_mv_done")
        s_rstd = sem("e_rstd_done")
        s_z = sem("e_z_done")
        s_zT_ps = sem("e_zT_ps")
        s_zT = sem("e_zT_done")
        s_gate_ps = sem("e_gate_ps")
        s_shift = sem("e_shift")
        s_exp = sem("e_exp")
        s_share = sem("e_share")
        s_up = sem("e_up")
        s_gelu = sem("e_gelu")
        s_y = sem("e_y_ps")
        s_yb = sem("e_yb")
        s_mix = sem("e_mix_done")
        s_res = sem("e_res_done")
        s_out = sem("e_out")

        PRESETS = 2
        block = ctx.enter_context(nc.Block())

        @block.sync
        def _(sp):
            for i in range(NCLS):
                r = 64 * (i % 2)
                sp.dma_start(hc[r:r + B, i // 2, :], h[i:i + 1, :, 0, :]).then_inc(s_in, 16)
            sp.dma_start(gate_w[:], dram["gate_w"]).then_inc(s_in, 16)
            sp.dma_start(b2[:], dram["e_b2"]).then_inc(s_in, 16)
            sp.wait_ge(s_res, NT)
            for i in range(NCLS):
                r = 64 * (i % 2)
                sp.dma_start(out[:, i, :], res[r:r + B, i // 2, :]).then_inc(s_out, 16)
            sp.wait_ge(s_out, 16 * NCLS)

        @block.gpsimd
        def _(pool):
            pool.memset(minus_half[:, :], -0.5).then_inc(s_preset, 1)
            pool.wait_ge(s_preset, PRESETS)
            pool.wait_ge(s_mv, NT)
            pool.tensor_scalar(veps[:, :], mv[:, :, 1], EPS, None, ALU.add).then_inc(s_rstd, 1)
            pool.wait_ge(s_rstd, 1)
            pool.tensor_tensor(rstd[:, :], veps[:, :], minus_half[:, :], ALU.pow).then_inc(s_rstd, 1)

        def tokens(a):
            if a < NT:
                return lambda part, k: zT[0:part, k, a * 128:(a + 1) * 128]
            return lambda part, k: zT[0:part, k, :].rearrange("p (t q b) -> p t q b", t=NT, q=2)[:, :, a - NT, :]

        @block.tensor
        def _(pe):
            pe.wait_ge(s_preset, PRESETS)
            pe.wait_ge(s_z, NT)
            for k in range(2):
                for t in range(NT):
                    mm = pe.transpose(ps_z[k][0:HF, t * 128:(t + 1) * 128], z[:, t, k * HF:(k + 1) * HF], ident[:, :])
            mm.then_inc(s_zT_ps, 1)
            pe.wait_ge(s_zT, 2)
            pe.wait_ge(s_in, 16 * (NCLS + 2))
            for t in range(NT):
                for k in range(2):
                    mm = pe.matmul(ps_gate[:, 4 * t:4 * t + 4], zT[0:HF, k, t * 128:(t + 1) * 128],
                                   gate_w[:, k, 4 * t:4 * t + 4], start=(k == 0), stop=(k == 1))
            mm.then_inc(s_gate_ps, 1)
            pe.wait_ge(s_experts, 32)
            n = 0
            for a in range(5):
                wide = WIDE[a]
                for u in range(FC // 2):
                    if n >= 2:
                        pe.wait_ge(s_gelu, n - 1)
                    for c in (2 * u, 2 * u + 1):
                        to = ps_up[n % 2][:, (c % 2) * wide:(c % 2 + 1) * wide]
                        pe.matmul(to, a1[:, a, 0, c * 128:(c + 1) * 128], tokens(a)(HF + 1, 0), start=True, stop=False)
                        mm = pe.matmul(to, a1[0:HF, a, 1, c * 128:(c + 1) * 128], tokens(a)(HF, 1),
                                       start=False, stop=True)
                    mm.then_inc(s_up, 1)
                    n += 1
            pe.wait_ge(s_gelu, n)
            for t in range(NT):
                for q in range(2):
                    for c in range(FC):
                        mm = pe.matmul(ps_y[t][64 * q:64 * q + 64, 0:D], hidden[:, c, 128 * t + 64 * q:128 * t + 64 * q + 64],
                                       a2[:, NT + q, c, :], start=(c == 0), stop=(c == FC - 1),
                                       tile_position=(0, 64 * q))
                mm.then_inc(s_y, 1)
                for c in range(FC):
                    second = hidden[:, c, (NT + t) * 128:(NT + t + 1) * 128]
                    mm = pe.matmul(ps_y[t][:, D:2 * D], second, a2[:, t, c, :], start=(c == 0), stop=(c == FC - 1))
                mm.then_inc(s_y, 1)

        @block.scalar
        def _(act):
            act.wait_ge(s_preset, PRESETS)
            act.wait_ge(s_zT_ps, 1)
            for k in range(2):
                act.activation(zT[0:HF, k, :], ps_z[k][0:HF, 0:NT * 128], ACT.Copy).then_inc(s_zT, 1)
            act.wait_ge(s_shift, 1)
            act.activation(expd[:, :, :], shifted[:, :, :], ACT.Exp).then_inc(s_exp, 1)
            n = 0
            for a in range(5):
                wide = WIDE[a]
                for u in range(FC // 2):
                    act.wait_ge(s_up, n + 1)
                    if a < NT:
                        to = hidden[:, 2 * u:2 * u + 2, 128 * a:128 * a + 128]
                        source = ps_up[n % 2][:, 0:2 * wide].rearrange("p (c t) -> p c t", c=2)
                    else:
                        to = hidden[:, 2 * u:2 * u + 2, 128 * NT:].rearrange("p c (t q b) -> p c t q b", t=NT, q=2)\
                            [:, :, :, a - NT, :]
                        source = ps_up[n % 2][:, 0:2 * wide].rearrange("p (c t b) -> p c t b", c=2, t=NT)
                    act.activation(to, source, ACT.Gelu).then_inc(s_gelu, 1)
                    n += 1

        @block.vector
        def _(dve):
            dve.memset(zT[HF:HF + 1, :, :], 1.0).then_inc(s_preset, 1)
            dve.wait_ge(s_in, 16 * (NCLS + 2))
            for t in range(NT):
                dve.bn_stats(stats[:, t, :], hc[:, t, :]).then_inc(s_stats, 1)
            dve.wait_ge(s_stats, NT)
            for t in range(NT):
                dve.bn_aggr(mv[:, t, :], stats[:, t, :]).then_inc(s_mv, 1)
            dve.wait_ge(s_rstd, 2)
            for t in range(NT):
                dve.tensor_scalar(z[:, t, :], hc[:, t, :], mv[:, t, 0:1], rstd[:, t:t + 1],
                                  ALU.subtract, ALU.mult).then_inc(s_z, 1)

            def pair(a):
                return a[:, :].rearrange("p (t o) -> p t o", o=1).broadcast_to([128, NT, 2])

            dve.wait_ge(s_gate_ps, 1)
            both = ps_gate[:, 0:4 * NT].rearrange("p (t q e) -> p t q e", t=NT, q=2)
            dve.tensor_copy(logits[0:64, :, :], both[0:64, :, 0, :]).then_inc(s_share, 1)
            dve.tensor_copy(logits[64:128, :, :], both[64:128, :, 1, :]).then_inc(s_share, 1)
            dve.wait_ge(s_share, 2)
            dve.tensor_tensor(top[:, :], logits[:, :, 0], logits[:, :, 1], ALU.max).then_inc(s_share, 1)
            dve.wait_ge(s_share, 3)
            dve.tensor_tensor(shifted[:, :, :], logits[:, :, :], pair(top), ALU.subtract).then_inc(s_shift, 1)
            dve.wait_ge(s_exp, 1)
            dve.tensor_tensor(total[:, :], expd[:, :, 0], expd[:, :, 1], ALU.add).then_inc(s_share, 1)
            dve.wait_ge(s_share, 4)
            dve.reciprocal(total_inv[:, :], total[:, :]).then_inc(s_share, 1)
            dve.wait_ge(s_share, 5)
            dve.tensor_tensor(gate[:, :, :], expd[:, :, :], pair(total_inv), ALU.mult).then_inc(s_share, 1)
            dve.wait_ge(s_share, 6)
            dve.tensor_tensor(least[:, :], gate[:, :, 0], gate[:, :, 1], ALU.min).then_inc(s_share, 1)
            dve.wait_ge(s_share, 7)
            dve.tensor_tensor(above[:, :, :], gate[:, :, :], pair(least), ALU.is_gt).then_inc(s_share, 1)
            dve.wait_ge(s_share, 8)
            dve.tensor_tensor(kept[:, :, :], gate[:, :, :], above[:, :, :], ALU.mult).then_inc(s_share, 1)
            dve.wait_ge(s_share, 9)
            dve.tensor_tensor(kept_sum[:, :], kept[:, :, 0], kept[:, :, 1], ALU.add).then_inc(s_share, 1)
            dve.wait_ge(s_share, 10)
            dve.tensor_scalar(kept_clip[:, :], kept_sum[:, :], 1e-6, None, ALU.max).then_inc(s_share, 1)
            dve.wait_ge(s_share, 11)
            dve.reciprocal(kept_inv[:, :], kept_clip[:, :]).then_inc(s_share, 1)
            dve.wait_ge(s_share, 12)
            dve.tensor_tensor(share[:, :, :], kept[:, :, :], pair(kept_inv), ALU.mult).then_inc(s_share, 1)
            dve.wait_ge(s_share, 13)
            for t in range(NT):
                dve.wait_ge(s_y, 2 * t + 2)
                dve.tensor_tensor(y[:, t, :, :], ps_y[t][:, 0:2 * D].rearrange("p (e d) -> p e d", e=2),
                                  b2[:, t, :, :], ALU.add).then_inc(s_yb, 1)
                dve.wait_ge(s_yb, t + 1)
                dve.scalar_tensor_tensor(out=mix[:, t, :], in0=y[:, t, 0, :], scalar=share[:, t, 0:1],
                                         in1=hc[:, t, :], op0=ALU.mult, op1=ALU.add).then_inc(s_mix, 1)
                dve.wait_ge(s_mix, t + 1)
                dve.scalar_tensor_tensor(out=res[:, t, :], in0=y[:, t, 1, :], scalar=share[:, t, 1:2],
                                         in1=mix[:, t, :], op0=ALU.mult, op1=ALU.add).then_inc(s_res, 1)


def vit_layer(nc, dram, out):
    with ExitStack() as ctx:
        h = ctx.enter_context(nc.sbuf_tensor("h", [128, B, 2, D], F32))
        ident = ctx.enter_context(nc.sbuf_tensor("identity", [128, 128], F32))
        phase_one(nc, h, ident, dram)
        a1 = ctx.enter_context(nc.sbuf_tensor("a1", [HF + 1, 5, 2, FF], F32))
        a2 = ctx.enter_context(nc.sbuf_tensor("a2", [128, 5, FC, D], F32))
        s_experts = ctx.enter_context(nc.semaphore("s_experts"))
        phase_two(nc, h, ident, dram, out, a1, a2, s_experts)
        phase_three(nc, h, ident, dram, out, a1, a2, s_experts)


def rope_tables():
    inv = (np.float32(1.0) / np.float32(10000.0) ** (np.arange(0, HD, 2, dtype=np.float32) / np.float32(HD)))
    angle = np.arange(T, dtype=np.float32)[:, None] * inv.astype(np.float32)[None, :]
    cos, sin = np.cos(angle), np.sin(angle)
    return np.concatenate([cos, cos], 1), np.concatenate([-sin, sin], 1)


def by_tiles(rows):
    full = np.zeros((2 * T0, rows.shape[1]), rows.dtype)
    full[:T] = rows
    return np.ascontiguousarray(full.reshape(2, T0, -1).transpose(1, 0, 2))


def in_chunks(w, bias=None):
    full = np.zeros((HF + 1, 2, w.shape[0]), w.dtype)
    full[:HF] = w.T.reshape(2, HF, -1).transpose(1, 0, 2)
    if bias is not None:
        full[HF, 0] = bias
    return full


def kernel(**inputs):
    import concourse.bacc as bacc
    from concourse.bass_utils import run_bass_kernel_spmd

    a = {k: np.asarray(v) for k, v in inputs.items()}
    f32 = np.float32
    patches = a["x"].reshape(B, 3, 14, 16, 14, 16).transpose(0, 1, 3, 5, 2, 4).reshape(B, KC, 128, T - 2)
    x = np.zeros((B, 128, KC, T), f32)
    x[:, :, :, 2:] = patches.transpose(0, 2, 1, 3)
    embed_a = np.concatenate([a["cls_tok"][0], a["L0_tok_cls_token"][0],
                              np.broadcast_to(a["L0_tok_conv_b"], (T - 2, D))])
    embed_b = np.concatenate([np.zeros((1, D), f32), a["L0_tok_pos_emb"][0]])
    cos, sin = rope_tables()
    later = np.where(np.arange(T)[None, :] > np.arange(T)[:, None], f32(FAR), f32(0))
    wq, wk, wv = (a[f"L0_attn_W{n}"] for n in "qkv")
    bqkv = np.concatenate([a[f"L0_attn_b{n}"] for n in "qkv"])
    a1 = np.stack([in_chunks(a["L0_ffn_A1_W"][n].T, a["L0_ffn_A1_b"][n]) for n in range(5)], 1)
    e_b2 = np.zeros((2, 64, NCLS // 2, 2, D), f32)
    for i, e, (_, c) in COMBOS:
        e_b2[i % 2, :, i // 2, e] = a["L0_ffn_A2_b"][c]
    gw = a["L0_ffn_G_W"].transpose(1, 0, 2).reshape(2, HF, 2 * NCLS).transpose(1, 0, 2)
    arrays = {
        "x": x.reshape(B, 128, KC * T),
        "conv_w": a["L0_tok_conv_w"].reshape(D, KC, 128).transpose(2, 1, 0),
        "embed_a": by_tiles(embed_a), "embed_b": by_tiles(embed_b),
        "wqkv": in_chunks(np.concatenate([wq, wk, wv]), bqkv),
        "wo": in_chunks(a["L0_attn_Wo"], a["L0_attn_bo"]),
        "cos": by_tiles(cos), "sin": by_tiles(sin),
        "mask0": later[:T0, :T0], "mask1": later[T0:],
        "ident": np.eye(128, dtype=f32),
        "w1": in_chunks(a["L0_ffn_moe0_W1"].T, a["L0_ffn_moe0_b1"]),
        "w2": a["L0_ffn_moe0_W2"].reshape(FC, 128, D).transpose(1, 0, 2),
        "b2": np.broadcast_to(a["L0_ffn_moe0_b2"], (128, D)),
        "a1": a1, "a2": a["L0_ffn_A2_W"].reshape(5, FC, 128, D).transpose(2, 0, 1, 3),
        "gate_w": gw, "e_b2": e_b2.reshape(128, NCLS // 2, 2, D),
    }
    arrays = {f"in_{k}": np.ascontiguousarray(v) for k, v in arrays.items()}
    nc = bacc.Bacc("TRN2", target_bir_lowering=False, num_devices=1)
    dram = {k[3:]: nc.dram_tensor(k, v.shape, F32, kind="ExternalInput").ap() for k, v in arrays.items()}
    out = nc.dram_tensor("out", [B, T, D], F32, kind="ExternalOutput").ap()
    vit_layer(nc, dram, out)
    result = run_bass_kernel_spmd(nc, [arrays], core_ids=[0])
    return result.results[0]["out"]
```

```python
from contextlib import ExitStack

import numpy as np

import concourse.bass as bass
from concourse import mybir

F32 = mybir.dt.float32
F32R = mybir.dt.float32r
ALU = mybir.AluOpType
ACT = mybir.ActivationFunctionType

B = 64
D = 192
T = 198
T0, T1 = 128, T - 128
TILES = ((0, T0), (T0, T1))
KC = 6
H, HD = 12, 16
VC = HD + 1
PAIRS = H // 2
HF = D // 2
FF = 768
FC = FF // 128
NCLS = 6
EPS = 1e-5
SCALE = HD ** -0.5
FAR = -1.0e30
TO_T, TO_PV = 3, 4
ROPE_ON_DVE = ()
ON_ACT = (0, 1, 2, 8)
CONV_AT = (0, 3, 5, 8, 8, 10, 10, 12, 12, 12, 12, 12, 12)
PAIRS_NEXT = {9: 0, 10: 1, 11: 2}
PAIRS_THIS = {0: 3, 2: 4, 3: 5}
PAIR_BANK = (0, 1, 0, 1, 1, 1)

GROUPS = ((0, 3), (0, 4), (1, 3), (1, 4), (2, 3), (2, 4))
COMBOS = [(i, e, (a, c) if e == 0 else (c, a)) for i, (a, c) in enumerate(GROUPS) for e in range(2)]


def live(m):
    return not isinstance(m, int) or 0 <= m < B


def after(engine, sem, count, all_of_them=None):
    if isinstance(count, int):
        if count <= 0:
            return
        count = count if all_of_them is None else min(count, all_of_them)
    engine.wait_ge(sem, count)


def over_images(engine, steps):
    for i in (-2, -1, 0, 1):
        steps(i)
    with engine.Fori(2, B - 2) as i:
        steps(i)
    for i in (B - 2, B - 1, B):
        steps(i)


def phase_one(nc, h, ident, dram):
    with ExitStack() as ctx:
        def sb(name, shape, dt=F32):
            return ctx.enter_context(nc.sbuf_tensor(name, shape, dt))

        def sem(name):
            return ctx.enter_context(nc.semaphore(name))

        conv_w = sb("conv_w", [128, KC, D])
        embed = sb("embed", [128, 2, D])
        embed_pos = sb("embed_pos", [128, 2, D])
        wqkv = sb("wqkv", [HF + 1, 2, 3 * D])
        wo = sb("wo", [HF + 1, 2, D])
        cos = sb("cos", [128, 2, HD])
        sin = sb("sin", [128, 2, HD])
        mask0 = sb("mask0", [128, T0])
        mask1 = sb("mask1", [T1, T])
        x = sb("x", [128, KC, T])
        stats = sb("stats", [128, 2, 6])
        mv = sb("mv", [128, 2, 2])
        veps = sb("veps", [128, 2])
        minus_half = sb("minus_half", [128, 2])
        eps = sb("eps", [128, 2])
        carrier = sb("carrier", [1, 16])
        zeros = sb("zeros", [128, 2, D])
        rstd = sb("rstd", [128, 2])
        z = sb("z", [128, 2, D])
        zT = sb("zT", [HF + 1, 2, T])
        rope_c = sb("rope_c", [128, 2, 2 * D])
        rope_s = sb("rope_s", [128, 2, 2 * D])
        rope = sb("rope", [128, 2, 2 * D])
        parts = sb("parts", [128, 2, 2, H, 4, HD], F32R)
        partsT = sb("partsT", [128, PAIRS, 2, T], F32R)
        v_stage = sb("v_stage", [128, 2, D])
        v = sb("v", [128, 2, H, VC])
        masked = sb("masked", [128, 3, T0 + T])
        negmax = sb("negmax", [128, H, 2])
        probs = sb("probs", [128, 4, T0 + T])
        probsT = sb("probsT", [128, 3, T + T1])
        rowsum_inv = sb("rowsum_inv", [128, 2, H])
        o = sb("o", [128, 2, D])
        onT = sb("onT", [HF + 1, 2, T])

        ps = [ctx.enter_context(nc.psum_tensor(f"ps{i}", [128, 512], F32)) for i in range(8)]
        ps_a, ps_b, ps_o, ps_c = ps[0], ps[1], ps[2], ps[3]
        ps_s = ps[4:6]
        ps_p = ps[6:8]

        s_const = sem("s_const")
        s_preset = sem("s_preset")
        s_embed = sem("s_embed")
        s_x = sem("s_x")
        s_conv = sem("s_conv")
        s_h0 = sem("s_h0")
        s_stats = sem("s_stats")
        s_mv = sem("s_mv")
        s_veps = sem("s_veps")
        s_rstd = sem("s_rstd")
        s_z = sem("s_z")
        s_zT_ps = sem("s_zT_ps")
        s_zT = sem("s_zT")
        s_qk = sem("s_qk")
        s_qk_read = sem("s_qk_read")
        s_rope = (sem("s_rope_0"), sem("s_rope_1"))
        s_hi = sem("s_hi")
        s_parts = sem("s_parts")
        s_v_ps = sem("s_v_ps")
        s_v_stage = sem("s_v_stage")
        s_v = sem("s_v")
        s_partsT_ps = sem("s_partsT_ps")
        s_partsT = sem("s_partsT")
        s_scores = sem("s_scores")
        s_masked = sem("s_masked")
        s_probs = sem("s_probs")
        s_pT_ps = sem("s_pT_ps")
        s_pT = sem("s_pT")
        s_pT_act = sem("s_pT_act")
        s_pv = sem("s_pv")
        s_rsum = sem("s_rsum")
        s_o = sem("s_o")
        s_onT_ps = sem("s_onT_ps")
        s_onT = sem("s_onT")
        s_wo = sem("s_wo")
        s_h1 = sem("s_h1")

        consts = [(conv_w, dram["conv_w"]), (embed, dram["embed_a"]), (embed_pos, dram["embed_b"]),
                  (wqkv, dram["wqkv"]), (wo, dram["wo"]), (cos, dram["cos"]), (sin, dram["sin"]),
                  (mask0, dram["mask0"]), (mask1, dram["mask1"]), (ident, dram["ident"])]
        PRESETS = 18

        on_dve = tuple(k for k in range(H) if k not in ON_ACT)

        def copied(i, k):
            sem_of, heads = (s_pT_act, ON_ACT) if k in ON_ACT else (s_pT, on_dve)
            return sem_of, i * len(heads) + heads.index(k) + 1

        def rope_sum(engine, m, t):
            n = TILES[t][1]
            after(engine, s_parts, m * 4 + 2 * t - 2)
            engine.tensor_tensor(rope[0:n, t, :], rope_c[0:n, t, :], rope_s[0:n, t, :], ALU.add)\
                .then_inc(s_rope[t], 1)

        def twice(t, w):
            n = TILES[t][1]
            return rope[0:n, t, w * D:(w + 1) * D].rearrange("p (h o d) -> p h o d", h=H, o=1)\
                .broadcast_to([n, H, 2, HD])

        def parts_of(t, w):
            blocks = parts[0:TILES[t][1], t, w, :, :, :]
            if w == 0:
                return blocks[:, :, 0:2, :], blocks[:, :, 2:4, :]
            return blocks[:, :, 0:4:2, :], blocks[:, :, 1:4:2, :]

        block = ctx.enter_context(nc.Block())

        @block.sync
        def _(sp):
            def load_x(m):
                after(sp, s_conv, m)
                sp.dma_start(x[:, :, :], dram["x"][bass.ds(m, 1)].rearrange("o p n -> p (o n)")
                             .rearrange("p (c t) -> p c t", c=KC)).then_inc(s_x, 16)

            load_x(0)
            for to, source in consts:
                sp.dma_start(to[:], source).then_inc(s_const, 16)
            with sp.Fori(1, B) as m:
                load_x(m)

        @block.gpsimd
        def _(pool):
            pool.memset(minus_half[:, :], -0.5).then_inc(s_preset, 1)
            pool.memset(eps[:, :], EPS).then_inc(s_preset, 1)
            pool.memset(mv[:, :, :], 1.0).then_inc(s_preset, 1)
            pool.memset(v[:, :, :, 0:HD], 0.0).then_inc(s_preset, 1)
            pool.memset(v[:, :, :, HD:HD + 1], 1.0).then_inc(s_preset, 1)
            pool.memset(v_stage[:, :, :], 0.0).then_inc(s_preset, 1)
            pool.memset(zeros[:, :, :], 0.0).then_inc(s_preset, 1)
            pool.wait_ge(s_preset, PRESETS)

            def rstd_of(m):
                pool.wait_ge(s_mv, m * 2 + 2)
                after(pool, s_z, m * 2)
                pool.tensor_tensor(veps[:, :], mv[:, :, 1], eps[:, :], ALU.add).then_inc(s_veps, 1)
                pool.wait_ge(s_veps, m + 1)
                pool.tensor_tensor(rstd[:, :], veps[:, :], minus_half[:, :], ALU.pow).then_inc(s_rstd, 1)

            def low_parts(m, t):
                if t not in ROPE_ON_DVE:
                    pool.wait_ge(s_qk_read, m * 2 + t + 1)
                    rope_sum(pool, m, t)
                pool.wait_ge(s_hi, m * 4 + 2 * t + 2)
                for w in range(2):
                    hi, lo = parts_of(t, w)
                    pool.tensor_tensor(lo, twice(t, w), hi.bitcast(F32), ALU.subtract).then_inc(s_parts, 1)

            def spread_v(m, g):
                pool.wait_ge(s_v_stage, m * 2 + 2)
                after(pool, s_pv, m * H - H + 4 * g + 4)
                four = slice(4 * g * HD, 4 * (g + 1) * HD)
                pool.tensor_tensor(v[:, :, 4 * g:4 * g + 4, 0:HD],
                                   v_stage[:, :, four].rearrange("p t (h d) -> p t h d", h=4),
                                   zeros[:, :, four].rearrange("p t (h d) -> p t h d", h=4), ALU.add)\
                    .then_inc(s_v, 1)

            def steps(i):
                if live(i + 1):
                    low_parts(i + 1, 0)
                    low_parts(i + 1, 1)
                    spread_v(i + 1, 0)
                if live(i + 2):
                    rstd_of(i + 2)
                if live(i + 1):
                    spread_v(i + 1, 1)
                    spread_v(i + 1, 2)

            over_images(pool, steps)

        @block.tensor
        def _(pe):
            def conv(m, first, last):
                for n in range(first, last):
                    t, c = n // KC, n % KC
                    at, rows = TILES[t]
                    if n == 0:
                        pe.wait_ge(s_x, m * 16 + 16)
                        after(pe, s_h0, m * 2)
                    mm = pe.matmul(ps_c[0:rows, t * D:(t + 1) * D], x[:, c, at:at + rows], conv_w[:, c, :],
                                   start=(c == 0), stop=(c == KC - 1))
                if last == 2 * KC:
                    mm.then_inc(s_conv, 1)

            def z_transpose(m):
                pe.wait_ge(s_z, m * 2 + 2)
                after(pe, s_partsT, m * PAIRS - 3)
                for t, (at, n) in enumerate(TILES):
                    for k in range(2):
                        mm = pe.transpose(ps_a[0:HF, k * T + at:k * T + at + n],
                                          z[0:n, t, k * HF:(k + 1) * HF], ident[0:n, 0:n])
                mm.then_inc(s_zT_ps, 1)

            def project(to, m, t, first, last):
                at, n = TILES[t]
                pe.matmul(to, zT[0:HF + 1, 0, at:at + n], wqkv[:, 0, first:last], start=True, stop=False)
                return pe.matmul(to, zT[0:HF, 1, at:at + n], wqkv[0:HF, 1, first:last], start=False, stop=True)

            def qk(m, t):
                n = TILES[t][1]
                if t == 0:
                    pe.wait_ge(s_zT, m + 1)
                else:
                    pe.wait_ge(s_qk_read, m * 2 + 1)
                project(ps_a[0:n, 0:2 * D], m, t, 0, 2 * D).then_inc(s_qk, 1)

            def values(m):
                pe.wait_ge(s_qk_read, m * 2 + 2)
                for t, (at, n) in enumerate(TILES):
                    mm = project(ps_a[0:n, t * D:(t + 1) * D], m, t, 2 * D, 3 * D)
                mm.then_inc(s_v_ps, 1)

            def parts_transpose(m, p):
                bank = (ps_a, ps_b)[PAIR_BANK[p]]
                if p == 0:
                    pe.wait_ge(s_parts, m * 4 + 4)
                    pe.wait_ge(s_v_stage, m * 2 + 2)
                elif p == 1:
                    after(pe, s_h1, m * 2 - 2, 2 * B)
                else:
                    pe.wait_ge(s_partsT, m * PAIRS + (p - 1 if p < 4 else p))
                for w in range(2):
                    for t, (at, n) in enumerate(TILES):
                        pair = parts[0:n, t, w, 2 * p:2 * p + 2, :, :].rearrange("p h b d -> p (h b d)")
                        mm = pe.transpose(bank[:, w * T + at:w * T + at + n], pair.bitcast(F32), ident[0:n, 0:n])
                mm.then_inc(s_partsT_ps, 1)

            def scores(i, k):
                p, r = k // 2, 64 * (k % 2)
                if k % 2 == 0:
                    pe.wait_ge(s_partsT, i * PAIRS + p + 1)
                after(pe, s_masked, i * H + k - 1)
                q, kk = partsT[r:r + 64, p, 0, :], partsT[r:r + 64, p, 1, :]
                bank = ps_s[k % 2]
                pe.matmul(bank[0:T0, 0:T0], q[:, 0:T0], kk[:, 0:T0], start=True, stop=True)
                pe.matmul(bank[0:T1, T0:T0 + T], q[:, T0:T], kk[:, 0:T], start=True, stop=True)\
                    .then_inc(s_scores, 1)

            def probs_transpose(i, k):
                pe.wait_ge(s_probs, i * H + k + 1)
                bank, p = ps_p[k % 2], probs[:, k % 4, :]
                pe.transpose(bank[0:T0, 0:T0], p[0:T0, 0:T0], ident[:, :])
                pe.transpose(bank[0:T0, T0:T], p[0:T1, T0:2 * T0], ident[0:T1, 0:T1])
                pe.transpose(bank[0:T1, T:T + T1], p[0:T1, 2 * T0:T0 + T], ident[0:T1, 0:T1])\
                    .then_inc(s_pT_ps, 1)

            def pv(i, k):
                pe.wait_ge(*copied(i, k))
                if k % 4 == 0:
                    pe.wait_ge(s_v, i * 3 + k // 4 + 1)
                if k == 0:
                    after(pe, s_o, i * 2)
                pT, values_of = probsT[:, k % 3, :], v[:, :, k, :]
                o0, o1 = (ps_o[0:n, (t * H + k) * VC:(t * H + k + 1) * VC] for t, (_, n) in enumerate(TILES))
                pe.matmul(o0, pT[:, 0:T0], values_of[:, 0, :], start=True, stop=True)
                pe.matmul(o1, pT[:, T0:T], values_of[:, 0, :], start=True, stop=False)
                pe.matmul(o1, pT[0:T1, T:T + T1], values_of[0:T1, 1, :], start=False, stop=True).then_inc(s_pv, 1)

            def on_transpose(b):
                pe.wait_ge(s_o, b * 2 + 2)
                after(pe, s_partsT, b * PAIRS + 2 * PAIRS, B * PAIRS)
                after(pe, s_h1, b * 2)
                for t, (at, n) in enumerate(TILES):
                    for k in range(2):
                        mm = pe.transpose(ps_b[0:HF, k * T + at:k * T + at + n],
                                          o[0:n, t, k * HF:(k + 1) * HF], ident[0:n, 0:n])
                mm.then_inc(s_onT_ps, 1)

            def out_project(b):
                pe.wait_ge(s_onT, b + 1)
                for t, (at, n) in enumerate(TILES):
                    to = ps_b[0:n, t * D:(t + 1) * D]
                    pe.matmul(to, onT[:, 0, at:at + n], wo[:, 0, :], start=True, stop=False)
                    mm = pe.matmul(to, onT[0:HF, 1, at:at + n], wo[0:HF, 1, :], start=False, stop=True)
                mm.then_inc(s_wo, 1)

            def steps(i):
                for k in range(H):
                    if live(i):
                        scores(i, k)
                    j, kk = (i, k - TO_PV) if k >= TO_PV else (i - 1, k - TO_PV + H)
                    if live(j):
                        pv(j, kk)
                    j, kk = (i, k - TO_T) if k >= TO_T else (i - 1, k - TO_T + H)
                    if live(j):
                        probs_transpose(j, kk)
                    if k in PAIRS_THIS and live(i):
                        parts_transpose(i, PAIRS_THIS[k])
                    if live(i + 1):
                        if k == 1:
                            z_transpose(i + 1)
                        if k in (3, 5):
                            qk(i + 1, (k - 3) // 2)
                        if k == 7:
                            values(i + 1)
                        if k in PAIRS_NEXT:
                            parts_transpose(i + 1, PAIRS_NEXT[k])
                    if live(i - 1):
                        if k == 5:
                            on_transpose(i - 1)
                        if k == 8:
                            out_project(i - 1)
                    if live(i + 2) and CONV_AT[k] < CONV_AT[k + 1]:
                        conv(i + 2, CONV_AT[k], CONV_AT[k + 1])

            pe.wait_ge(s_const, 16 * len(consts))
            pe.wait_ge(s_preset, PRESETS)
            over_images(pe, steps)

        @block.scalar
        def _(act):
            act.wait_ge(s_preset, PRESETS)

            def exps(i, k):
                act.wait_ge(s_masked, i * H + k + 1)
                after(act, s_pT_ps, i * H + k - 3)
                act.activation(probs[0:T0, k % 4, 0:T0], masked[0:T0, k % 3, 0:T0], ACT.Exp,
                               bias=negmax[0:T0, k, 0:1], scale=-1.0)
                act.activation(probs[0:T1, k % 4, T0:T0 + T], masked[0:T1, k % 3, T0:T0 + T], ACT.Exp,
                               bias=negmax[0:T1, k, 1:2], scale=-1.0).then_inc(s_probs, 1)

            def probs_copy(i, k):
                act.wait_ge(s_pT_ps, i * H + k + 1)
                act.activation(probsT[:, k % 3, :], ps_p[k % 2][:, 0:T + T1], ACT.Copy).then_inc(s_pT_act, 1)

            def z_copy(m):
                act.wait_ge(s_zT_ps, m + 1)
                after(act, s_v_ps, m)
                act.activation(zT[0:HF, :, :], ps_a[0:HF, 0:2 * T].rearrange("p (k t) -> p k t", k=2), ACT.Copy)\
                    .then_inc(s_zT, 1)

            def on_copy(b):
                act.wait_ge(s_onT_ps, b + 1)
                after(act, s_wo, b)
                act.activation(onT[0:HF, :, :], ps_b[0:HF, 0:2 * T].rearrange("p (k t) -> p k t", k=2), ACT.Copy)\
                    .then_inc(s_onT, 1)

            def v_copy(m):
                act.wait_ge(s_v_ps, m + 1)
                after(act, s_v, m * 3)
                for t, (at, n) in enumerate(TILES):
                    act.activation(v_stage[0:n, t, :], ps_a[0:n, t * D:(t + 1) * D], ACT.Copy)\
                        .then_inc(s_v_stage, 1)

            def parts_copy(m, p):
                act.wait_ge(s_partsT_ps, m * PAIRS + p + 1)
                after(act, s_scores, m * H - H + 2 * p + 2)
                bank = (ps_a, ps_b)[PAIR_BANK[p]]
                act.activation(partsT[:, p, :, :], bank[:, 0:2 * T].rearrange("p (w t) -> p w t", w=2), ACT.Copy)\
                    .then_inc(s_partsT, 1)

            def high_parts(m, t):
                n = TILES[t][1]
                act.wait_ge(s_rope[t], m + 1)
                after(act, s_partsT_ps, m * PAIRS)
                for w in range(2):
                    act.activation(parts_of(t, w)[0], twice(t, w), ACT.Copy).then_inc(s_hi, 1)

            def steps(i):
                for k in range(H):
                    j, kk = (i, k - TO_T) if k >= TO_T else (i - 1, k - TO_T + H)
                    if live(j) and kk in ON_ACT:
                        probs_copy(j, kk)
                    if live(i):
                        exps(i, k)
                    if k in PAIRS_THIS and live(i):
                        parts_copy(i, PAIRS_THIS[k])
                    if live(i + 1):
                        if k == 1:
                            z_copy(i + 1)
                        if k in (5, 7):
                            high_parts(i + 1, (k - 5) // 2)
                        if k == 7:
                            v_copy(i + 1)
                        if k in PAIRS_NEXT:
                            parts_copy(i + 1, PAIRS_NEXT[k])
                    if live(i - 1):
                        if k == 5:
                            on_copy(i - 1)

            over_images(act, steps)

        @block.vector
        def _(dve):
            dve.memset(zT[HF:HF + 1, :, :], 1.0).then_inc(s_preset, 1)
            dve.memset(onT[HF:HF + 1, :, :], 1.0).then_inc(s_preset, 1)
            for bank in ps:
                dve.memset(bank[:, :], 0.0).then_inc(s_preset, 1)
            dve.wait_ge(s_const, 16 * len(consts))
            dve.tensor_tensor(embed[:, :, :], embed[:, :, :], embed_pos[:, :, :], ALU.add).then_inc(s_preset, 1)
            dve.wait_ge(s_preset, PRESETS)

            def probs_copy(i, k):
                dve.wait_ge(s_pT_ps, i * H + k + 1)
                dve.tensor_copy(probsT[:, k % 3, :], ps_p[k % 2][:, 0:T + T1]).then_inc(s_pT, 1)

            def row_max(i, k):
                bank = ps_s[k % 2]
                dve.tensor_tensor_reduce(masked[0:T0, k % 3, 0:T0], bank[0:T0, 0:T0], mask0[:, :], -SCALE, 1e38,
                                         ALU.add, ALU.min, negmax[0:T0, k, 0:1])
                dve.tensor_tensor_reduce(masked[0:T1, k % 3, T0:T0 + T], bank[0:T1, T0:T0 + T], mask1[:, :], -SCALE,
                                         1e38, ALU.add, ALU.min, negmax[0:T1, k, 1:2]).then_inc(s_masked, 1)

            def h_tile(m, t, n):
                return h[0:n, bass.ds(m, 1), t, :].rearrange("p o d -> p (o d)")

            def embed_add(m):
                dve.wait_ge(s_conv, m + 1)
                for t, (at, n) in enumerate(TILES):
                    dve.tensor_tensor(h_tile(m, t, n), ps_c[0:n, t * D:(t + 1) * D], embed[0:n, t, :], ALU.add)\
                        .then_inc(s_h0, 1)

            def moments(m):
                dve.wait_ge(s_h0, m * 2 + 2)
                dve.memset(carrier[:, 12:13], 0.0)
                for t, (at, n) in enumerate(TILES):
                    dve.bn_stats(stats[0:n, t, :], h_tile(m, t, n)).then_inc(s_stats, 1)

            def aggregate(m):
                dve.wait_ge(s_stats, m * 2 + 2)
                after(dve, s_rstd, m)
                dve.memset(carrier[:, 13:14], 0.0)
                for t, (at, n) in enumerate(TILES):
                    dve.bn_aggr(mv[0:n, t, :], stats[0:n, t, :]).then_inc(s_mv, 1)

            def normalise(m):
                dve.wait_ge(s_rstd, m + 1)
                after(dve, s_zT_ps, m)
                for t, (at, n) in enumerate(TILES):
                    dve.tensor_scalar(z[0:n, t, :], h_tile(m, t, n), mv[0:n, t, 0:1], rstd[0:n, t:t + 1],
                                      ALU.subtract, ALU.mult).then_inc(s_z, 1)

            def rotate(m, t):
                n = TILES[t][1]
                dve.wait_ge(s_qk, m * 2 + t + 1)
                if t not in ROPE_ON_DVE:
                    after(dve, s_parts, m * 4 + 2 * t - 2)
                heads = ps_a[0:n, 0:2 * D].rearrange("p (h d) -> p h d", d=HD)
                to_c = rope_c[0:n, t, :].rearrange("p (h d) -> p h d", d=HD)
                to_s = rope_s[0:n, t, :].rearrange("p (h d) -> p h d", d=HD)
                half = HD // 2

                def table(which, a, b):
                    return which[0:n, t, a:b].rearrange("p (o d) -> p o d", o=1).broadcast_to([n, 2 * H, b - a])

                dve.tensor_tensor(to_c, heads, table(cos, 0, HD), ALU.mult)
                dve.tensor_tensor(to_s[:, :, 0:half], heads[:, :, half:HD], table(sin, 0, half), ALU.mult)
                dve.tensor_tensor(to_s[:, :, half:HD], heads[:, :, 0:half], table(sin, half, HD), ALU.mult)\
                    .then_inc(s_qk_read, 1)
                if t in ROPE_ON_DVE:
                    dve.wait_ge(s_qk_read, m * 2 + t + 1)
                    rope_sum(dve, m, t)

            def o_normalise(b):
                dve.wait_ge(s_pv, b * H + H)
                heads = [ps_o[0:n, t * H * VC:(t + 1) * H * VC].rearrange("p (h d) -> p h d", d=VC)
                         for t, (_, n) in enumerate(TILES)]
                for t, (_, n) in enumerate(TILES):
                    dve.reciprocal(rowsum_inv[0:n, t, :], heads[t][:, :, HD]).then_inc(s_rsum, 1)
                dve.wait_ge(s_rsum, b * 2 + 2)
                after(dve, s_onT_ps, b)
                for t, (_, n) in enumerate(TILES):
                    dve.tensor_tensor(o[0:n, t, :].rearrange("p (h d) -> p h d", d=HD), heads[t][:, :, 0:HD],
                                      rowsum_inv[0:n, t, :].rearrange("p (h o) -> p h o", o=1)
                                      .broadcast_to([n, H, HD]), ALU.mult).then_inc(s_o, 1)

            def residual(b):
                dve.wait_ge(s_wo, b + 1)
                for t, (at, n) in enumerate(TILES):
                    dve.tensor_tensor(h_tile(b, t, n), h_tile(b, t, n), ps_b[0:n, t * D:(t + 1) * D], ALU.add)\
                        .then_inc(s_h1, 1)

            def steps(i):
                for k in range(H):
                    if live(i):
                        after(dve, s_probs, i * H + k - 2)
                        dve.wait_ge(s_scores, i * H + k + 1)
                    j, kk = (i, k - TO_T) if k >= TO_T else (i - 1, k - TO_T + H)
                    if live(j) and kk in on_dve:
                        probs_copy(j, kk)
                    elif live(i):
                        dve.memset(carrier[:, k:k + 1], 0.0)
                    if live(i):
                        row_max(i, k)
                    if live(i - 1):
                        if k == 3:
                            o_normalise(i - 1)
                        if k == 8:
                            residual(i - 1)
                    if live(i + 2):
                        if k == 7:
                            embed_add(i + 2)
                        if k == 9:
                            moments(i + 2)
                        if k == 11:
                            aggregate(i + 2)
                    if live(i + 1):
                        if k == 0:
                            normalise(i + 1)
                        if k in (3, 5):
                            rotate(i + 1, (k - 3) // 2)

            over_images(dve, steps)


def phase_two(nc, h, ident, dram, out, a1, a2, s_experts):
    with ExitStack() as ctx:
        def sb(name, shape, dt=F32):
            return ctx.enter_context(nc.sbuf_tensor(name, shape, dt))

        def sem(name):
            return ctx.enter_context(nc.semaphore(name))

        w1 = sb("w1", [HF + 1, 2, FF])
        w2 = sb("w2", [128, FC, D])
        b2 = sb("b2", [128, D])
        stats = sb("f_stats", [128, 2, 6])
        mv = sb("f_mv", [128, 2, 2])
        veps = sb("f_veps", [128, 2])
        minus_half = sb("f_minus_half", [128, 2])
        eps = sb("f_eps", [128, 2])
        carrier = sb("f_carrier", [1, 2])
        rstd = sb("f_rstd", [128, 2])
        z = sb("f_z", [128, 2, D])
        zT = sb("f_zT", [HF + 1, 2, T])
        hidden = sb("hidden", [128, FC, T])
        h_b2 = sb("h_b2", [128, 2, D])
        result = sb("result", [128, 2, D])

        ps = [ctx.enter_context(nc.psum_tensor(f"f_ps{i}", [128, 512], F32)) for i in range(6)]
        ps_up, ps_z, ps_down = ps[0:3], ps[3], ps[4:6]

        s_w = sem("f_w")
        s_preset = sem("f_preset")
        s_stats = sem("f_stats_done")
        s_mv = sem("f_mv_done")
        s_veps = sem("f_veps_done")
        s_rstd = sem("f_rstd_done")
        s_z = sem("f_z_done")
        s_zT_ps = sem("f_zT_ps")
        s_zT = sem("f_zT_done")
        s_up = sem("f_up")
        s_gelu = sem("f_gelu")
        s_down = sem("f_down")
        s_hb = sem("f_hb")
        s_result = sem("f_result")
        s_stored = sem("f_stored")

        loads = [(w1, dram["w1"]), (w2, dram["w2"]), (b2, dram["b2"])]
        PRESETS = 4
        block = ctx.enter_context(nc.Block())

        @block.sync
        def _(sp):
            for to, source in loads:
                sp.dma_start(to[:], source).then_inc(s_w, 16)
            sp.dma_start(a1[:], dram["a1"]).then_inc(s_experts, 16)
            sp.dma_start(a2[:], dram["a2"]).then_inc(s_experts, 16)
            with sp.Fori(0, B) as j:
                sp.wait_ge(s_result, j * 2 + 1)
                sp.dma_start(out[bass.ds(j, 1), NCLS:T0, :].rearrange("o p d -> p (o d)"), result[NCLS:T0, 0, :])\
                    .then_inc(s_stored, 16)
                sp.wait_ge(s_result, j * 2 + 2)
                sp.dma_start(out[bass.ds(j, 1), T0:T, :].rearrange("o p d -> p (o d)"), result[0:T1, 1, :])\
                    .then_inc(s_stored, 16)
            sp.wait_ge(s_stored, 32 * B)

        def h_tile(m, t, n):
            return h[0:n, bass.ds(m, 1), t, :].rearrange("p o d -> p (o d)")

        @block.gpsimd
        def _(pool):
            pool.memset(minus_half[:, :], -0.5).then_inc(s_preset, 1)
            pool.memset(eps[:, :], EPS).then_inc(s_preset, 1)
            pool.memset(mv[:, :, :], 1.0).then_inc(s_preset, 1)
            pool.wait_ge(s_preset, PRESETS)
            pool.wait_ge(s_w, 16 * len(loads))

            def image(j, first):
                if not first:
                    pool.wait_ge(s_z, j * 2)
                pool.wait_ge(s_mv, j * 2 + 2)
                pool.tensor_tensor(veps[:, :], mv[:, :, 1], eps[:, :], ALU.add).then_inc(s_veps, 1)
                pool.wait_ge(s_veps, j + 1)
                pool.tensor_tensor(rstd[:, :], veps[:, :], minus_half[:, :], ALU.pow).then_inc(s_rstd, 1)
                if not first:
                    pool.wait_ge(s_result, j * 2)
                for t, (at, n) in enumerate(TILES):
                    pool.tensor_tensor(h_b2[0:n, t, :], h_tile(j, t, n), b2[0:n, :], ALU.add).then_inc(s_hb, 1)

            image(0, True)
            with pool.Fori(1, B) as j:
                image(j, False)

        @block.tensor
        def _(pe):
            pe.wait_ge(s_preset, PRESETS)
            pe.wait_ge(s_w, 16 * len(loads))

            def transpose_z(j):
                pe.wait_ge(s_z, j * 2 + 2)
                for t, (at, n) in enumerate(TILES):
                    for k in range(2):
                        mm = pe.transpose(ps_z[0:HF, k * T + at:k * T + at + n],
                                          z[0:n, t, k * HF:(k + 1) * HF], ident[0:n, 0:n])
                mm.then_inc(s_zT_ps, 1)

            def up(j, first):
                pe.wait_ge(s_zT, j + 1)
                for u in range(FC // 2):
                    if not first:
                        pe.wait_ge(s_gelu, j * 3 - 2 + u)
                    for c in (2 * u, 2 * u + 1):
                        to = ps_up[u][:, (c % 2) * T:(c % 2 + 1) * T]
                        pe.matmul(to, w1[:, 0, c * 128:(c + 1) * 128], zT[:, 0, :], start=True, stop=False)
                        mm = pe.matmul(to, w1[0:HF, 1, c * 128:(c + 1) * 128], zT[0:HF, 1, :],
                                       start=False, stop=True)
                    mm.then_inc(s_up, 1)

            def down(j, first):
                for t, (at, n) in enumerate(TILES):
                    if not first:
                        pe.wait_ge(s_result, j * 2 - 1 + t)
                    for c in range(FC):
                        if t == 0 and c % 2 == 0:
                            pe.wait_ge(s_gelu, j * 3 + c // 2 + 1)
                        mm = pe.matmul(ps_down[t][0:n, 0:D], hidden[:, c, at:at + n], w2[:, c, :],
                                       start=(c == 0), stop=(c == FC - 1))
                    mm.then_inc(s_down, 1)

            def image(j, first=False, last=False):
                up(j, first)
                if not last:
                    transpose_z(j + 1)
                down(j, first)

            transpose_z(0)
            image(0, first=True)
            with pe.Fori(1, B - 1) as j:
                image(j)
            image(B - 1, last=True)

        @block.scalar
        def _(act):
            act.wait_ge(s_preset, PRESETS)

            def z_copy(j, first):
                act.wait_ge(s_zT_ps, j + 1)
                if not first:
                    act.wait_ge(s_up, j * 3)
                act.activation(zT[0:HF, :, :], ps_z[0:HF, 0:2 * T].rearrange("p (k t) -> p k t", k=2), ACT.Copy)\
                    .then_inc(s_zT, 1)

            def gelus(j, first):
                for u in range(FC // 2):
                    act.wait_ge(s_up, j * 3 + u + 1)
                    if not first:
                        act.wait_ge(s_down, j * 2)
                    act.activation(hidden[:, 2 * u:2 * u + 2, :],
                                   ps_up[u][:, 0:2 * T].rearrange("p (c t) -> p c t", c=2), ACT.Gelu)\
                        .then_inc(s_gelu, 1)

            z_copy(0, True)
            gelus(0, True)
            z_copy(1, False)
            with act.Fori(1, B - 1) as j:
                gelus(j, False)
                z_copy(j + 1, False)
            gelus(B - 1, False)

        @block.vector
        def _(dve):
            dve.memset(zT[HF:HF + 1, :, :], 1.0).then_inc(s_preset, 1)
            dve.wait_ge(s_preset, PRESETS)

            def normalise(j, first):
                for t, (at, n) in enumerate(TILES):
                    dve.bn_stats(stats[0:n, t, :], h_tile(j, t, n)).then_inc(s_stats, 1)
                if not first:
                    dve.wait_ge(s_rstd, j)
                dve.wait_ge(s_stats, j * 2 + 2)
                dve.memset(carrier[:, 0:1], 0.0)
                for t, (at, n) in enumerate(TILES):
                    dve.bn_aggr(mv[0:n, t, :], stats[0:n, t, :]).then_inc(s_mv, 1)
                dve.wait_ge(s_rstd, j + 1)
                if not first:
                    dve.wait_ge(s_zT_ps, j)
                for t, (at, n) in enumerate(TILES):
                    dve.tensor_scalar(z[0:n, t, :], h_tile(j, t, n), mv[0:n, t, 0:1], rstd[0:n, t:t + 1],
                                      ALU.subtract, ALU.mult).then_inc(s_z, 1)

            def finish(j, first):
                for t, (at, n) in enumerate(TILES):
                    dve.wait_ge(s_down, j * 2 + t + 1)
                    dve.wait_ge(s_hb, j * 2 + t + 1)
                    if not first:
                        dve.wait_ge(s_stored, j * 32)
                    dve.tensor_tensor(result[0:n, t, :], ps_down[t][0:n, 0:D], h_b2[0:n, t, :], ALU.add)\
                        .then_inc(s_result, 1)

            normalise(0, True)
            normalise(1, False)
            finish(0, True)
            with dve.Fori(1, B - 1) as j:
                normalise(j + 1, False)
                finish(j, False)
            finish(B - 1, False)


def phase_three(nc, h, ident, dram, out, a1, a2, s_experts):
    NT = NCLS // 2
    WIDE = [128] * NT + [64 * NT] * 2

    with ExitStack() as ctx:
        def sb(name, shape, dt=F32):
            return ctx.enter_context(nc.sbuf_tensor(name, shape, dt))

        def sem(name):
            return ctx.enter_context(nc.semaphore(name))

        gate_w = sb("gate_w", [HF, 2, 2 * NCLS])
        b2 = sb("e_b2", [128, NT, 2, D])
        hc = sb("hc", [128, NT, D])
        stats = sb("e_stats", [128, NT, 6])
        mv = sb("e_mv", [128, NT, 2])
        veps = sb("e_veps", [128, NT])
        minus_half = sb("e_minus_half", [128, NT])
        rstd = sb("e_rstd", [128, NT])
        z = sb("e_z", [128, NT, D])
        zT = sb("e_zT", [HF + 1, 2, NT * 128])
        hidden = sb("e_hidden", [128, FC, 2 * NT * 128])
        logits = sb("logits", [128, NT, 2])
        top = sb("top", [128, NT])
        shifted = sb("shifted", [128, NT, 2])
        expd = sb("expd", [128, NT, 2])
        total = sb("total", [128, NT])
        total_inv = sb("total_inv", [128, NT])
        gate = sb("gate", [128, NT, 2])
        least = sb("least", [128, NT])
        above = sb("above", [128, NT, 2])
        kept = sb("kept", [128, NT, 2])
        kept_sum = sb("kept_sum", [128, NT])
        kept_clip = sb("kept_clip", [128, NT])
        kept_inv = sb("kept_inv", [128, NT])
        share = sb("share", [128, NT, 2])
        y = sb("e_y", [128, NT, 2, D])
        mix = sb("e_mix", [128, NT, D])
        res = sb("e_res", [128, NT, D])

        ps = [ctx.enter_context(nc.psum_tensor(f"e_ps{i}", [128, 512], F32)) for i in range(8)]
        ps_z, ps_gate, ps_up, ps_y = ps[0:2], ps[2], ps[3:5], ps[5:8]

        s_in = sem("e_in")
        s_preset = sem("e_preset")
        s_stats = sem("e_stats_done")
        s_mv = sem("e_mv_done")
        s_rstd = sem("e_rstd_done")
        s_z = sem("e_z_done")
        s_zT_ps = sem("e_zT_ps")
        s_zT = sem("e_zT_done")
        s_gate_ps = sem("e_gate_ps")
        s_shift = sem("e_shift")
        s_exp = sem("e_exp")
        s_share = sem("e_share")
        s_up = sem("e_up")
        s_gelu = sem("e_gelu")
        s_y = sem("e_y_ps")
        s_yb = sem("e_yb")
        s_mix = sem("e_mix_done")
        s_res = sem("e_res_done")
        s_out = sem("e_out")

        PRESETS = 2
        block = ctx.enter_context(nc.Block())

        @block.sync
        def _(sp):
            for i in range(NCLS):
                r = 64 * (i % 2)
                sp.dma_start(hc[r:r + B, i // 2, :], h[i:i + 1, :, 0, :]).then_inc(s_in, 16)
            sp.dma_start(gate_w[:], dram["gate_w"]).then_inc(s_in, 16)
            sp.dma_start(b2[:], dram["e_b2"]).then_inc(s_in, 16)
            sp.wait_ge(s_res, NT)
            for i in range(NCLS):
                r = 64 * (i % 2)
                sp.dma_start(out[:, i, :], res[r:r + B, i // 2, :]).then_inc(s_out, 16)
            sp.wait_ge(s_out, 16 * NCLS)

        @block.gpsimd
        def _(pool):
            pool.memset(minus_half[:, :], -0.5).then_inc(s_preset, 1)
            pool.wait_ge(s_preset, PRESETS)
            pool.wait_ge(s_mv, NT)
            pool.tensor_scalar(veps[:, :], mv[:, :, 1], EPS, None, ALU.add).then_inc(s_rstd, 1)
            pool.wait_ge(s_rstd, 1)
            pool.tensor_tensor(rstd[:, :], veps[:, :], minus_half[:, :], ALU.pow).then_inc(s_rstd, 1)

        def tokens(a):
            if a < NT:
                return lambda part, k: zT[0:part, k, a * 128:(a + 1) * 128]
            return lambda part, k: zT[0:part, k, :].rearrange("p (t q b) -> p t q b", t=NT, q=2)[:, :, a - NT, :]

        @block.tensor
        def _(pe):
            pe.wait_ge(s_preset, PRESETS)
            pe.wait_ge(s_z, NT)
            for k in range(2):
                for t in range(NT):
                    mm = pe.transpose(ps_z[k][0:HF, t * 128:(t + 1) * 128], z[:, t, k * HF:(k + 1) * HF], ident[:, :])
            mm.then_inc(s_zT_ps, 1)
            pe.wait_ge(s_zT, 2)
            pe.wait_ge(s_in, 16 * (NCLS + 2))
            for t in range(NT):
                for k in range(2):
                    mm = pe.matmul(ps_gate[:, 4 * t:4 * t + 4], zT[0:HF, k, t * 128:(t + 1) * 128],
                                   gate_w[:, k, 4 * t:4 * t + 4], start=(k == 0), stop=(k == 1))
            mm.then_inc(s_gate_ps, 1)
            pe.wait_ge(s_experts, 32)
            n = 0
            for a in range(5):
                wide = WIDE[a]
                for u in range(FC // 2):
                    if n >= 2:
                        pe.wait_ge(s_gelu, n - 1)
                    for c in (2 * u, 2 * u + 1):
                        to = ps_up[n % 2][:, (c % 2) * wide:(c % 2 + 1) * wide]
                        pe.matmul(to, a1[:, a, 0, c * 128:(c + 1) * 128], tokens(a)(HF + 1, 0), start=True, stop=False)
                        mm = pe.matmul(to, a1[0:HF, a, 1, c * 128:(c + 1) * 128], tokens(a)(HF, 1),
                                       start=False, stop=True)
                    mm.then_inc(s_up, 1)
                    n += 1
            pe.wait_ge(s_gelu, n)
            for t in range(NT):
                for q in range(2):
                    for c in range(FC):
                        mm = pe.matmul(ps_y[t][64 * q:64 * q + 64, 0:D], hidden[:, c, 128 * t + 64 * q:128 * t + 64 * q + 64],
                                       a2[:, NT + q, c, :], start=(c == 0), stop=(c == FC - 1),
                                       tile_position=(0, 64 * q))
                mm.then_inc(s_y, 1)
                for c in range(FC):
                    second = hidden[:, c, (NT + t) * 128:(NT + t + 1) * 128]
                    mm = pe.matmul(ps_y[t][:, D:2 * D], second, a2[:, t, c, :], start=(c == 0), stop=(c == FC - 1))
                mm.then_inc(s_y, 1)

        @block.scalar
        def _(act):
            act.wait_ge(s_preset, PRESETS)
            act.wait_ge(s_zT_ps, 1)
            for k in range(2):
                act.activation(zT[0:HF, k, :], ps_z[k][0:HF, 0:NT * 128], ACT.Copy).then_inc(s_zT, 1)
            act.wait_ge(s_shift, 1)
            act.activation(expd[:, :, :], shifted[:, :, :], ACT.Exp).then_inc(s_exp, 1)
            n = 0
            for a in range(5):
                wide = WIDE[a]
                for u in range(FC // 2):
                    act.wait_ge(s_up, n + 1)
                    if a < NT:
                        to = hidden[:, 2 * u:2 * u + 2, 128 * a:128 * a + 128]
                        source = ps_up[n % 2][:, 0:2 * wide].rearrange("p (c t) -> p c t", c=2)
                    else:
                        to = hidden[:, 2 * u:2 * u + 2, 128 * NT:].rearrange("p c (t q b) -> p c t q b", t=NT, q=2)\
                            [:, :, :, a - NT, :]
                        source = ps_up[n % 2][:, 0:2 * wide].rearrange("p (c t b) -> p c t b", c=2, t=NT)
                    act.activation(to, source, ACT.Gelu).then_inc(s_gelu, 1)
                    n += 1

        @block.vector
        def _(dve):
            dve.memset(zT[HF:HF + 1, :, :], 1.0).then_inc(s_preset, 1)
            dve.wait_ge(s_in, 16 * (NCLS + 2))
            for t in range(NT):
                dve.bn_stats(stats[:, t, :], hc[:, t, :]).then_inc(s_stats, 1)
            dve.wait_ge(s_stats, NT)
            for t in range(NT):
                dve.bn_aggr(mv[:, t, :], stats[:, t, :]).then_inc(s_mv, 1)
            dve.wait_ge(s_rstd, 2)
            for t in range(NT):
                dve.tensor_scalar(z[:, t, :], hc[:, t, :], mv[:, t, 0:1], rstd[:, t:t + 1],
                                  ALU.subtract, ALU.mult).then_inc(s_z, 1)

            def pair(a):
                return a[:, :].rearrange("p (t o) -> p t o", o=1).broadcast_to([128, NT, 2])

            dve.wait_ge(s_gate_ps, 1)
            both = ps_gate[:, 0:4 * NT].rearrange("p (t q e) -> p t q e", t=NT, q=2)
            dve.tensor_copy(logits[0:64, :, :], both[0:64, :, 0, :]).then_inc(s_share, 1)
            dve.tensor_copy(logits[64:128, :, :], both[64:128, :, 1, :]).then_inc(s_share, 1)
            dve.wait_ge(s_share, 2)
            dve.tensor_tensor(top[:, :], logits[:, :, 0], logits[:, :, 1], ALU.max).then_inc(s_share, 1)
            dve.wait_ge(s_share, 3)
            dve.tensor_tensor(shifted[:, :, :], logits[:, :, :], pair(top), ALU.subtract).then_inc(s_shift, 1)
            dve.wait_ge(s_exp, 1)
            dve.tensor_tensor(total[:, :], expd[:, :, 0], expd[:, :, 1], ALU.add).then_inc(s_share, 1)
            dve.wait_ge(s_share, 4)
            dve.reciprocal(total_inv[:, :], total[:, :]).then_inc(s_share, 1)
            dve.wait_ge(s_share, 5)
            dve.tensor_tensor(gate[:, :, :], expd[:, :, :], pair(total_inv), ALU.mult).then_inc(s_share, 1)
            dve.wait_ge(s_share, 6)
            dve.tensor_tensor(least[:, :], gate[:, :, 0], gate[:, :, 1], ALU.min).then_inc(s_share, 1)
            dve.wait_ge(s_share, 7)
            dve.tensor_tensor(above[:, :, :], gate[:, :, :], pair(least), ALU.is_gt).then_inc(s_share, 1)
            dve.wait_ge(s_share, 8)
            dve.tensor_tensor(kept[:, :, :], gate[:, :, :], above[:, :, :], ALU.mult).then_inc(s_share, 1)
            dve.wait_ge(s_share, 9)
            dve.tensor_tensor(kept_sum[:, :], kept[:, :, 0], kept[:, :, 1], ALU.add).then_inc(s_share, 1)
            dve.wait_ge(s_share, 10)
            dve.tensor_scalar(kept_clip[:, :], kept_sum[:, :], 1e-6, None, ALU.max).then_inc(s_share, 1)
            dve.wait_ge(s_share, 11)
            dve.reciprocal(kept_inv[:, :], kept_clip[:, :]).then_inc(s_share, 1)
            dve.wait_ge(s_share, 12)
            dve.tensor_tensor(share[:, :, :], kept[:, :, :], pair(kept_inv), ALU.mult).then_inc(s_share, 1)
            dve.wait_ge(s_share, 13)
            for t in range(NT):
                dve.wait_ge(s_y, 2 * t + 2)
                dve.tensor_tensor(y[:, t, :, :], ps_y[t][:, 0:2 * D].rearrange("p (e d) -> p e d", e=2),
                                  b2[:, t, :, :], ALU.add).then_inc(s_yb, 1)
                dve.wait_ge(s_yb, t + 1)
                dve.scalar_tensor_tensor(out=mix[:, t, :], in0=y[:, t, 0, :], scalar=share[:, t, 0:1],
                                         in1=hc[:, t, :], op0=ALU.mult, op1=ALU.add).then_inc(s_mix, 1)
                dve.wait_ge(s_mix, t + 1)
                dve.scalar_tensor_tensor(out=res[:, t, :], in0=y[:, t, 1, :], scalar=share[:, t, 1:2],
                                         in1=mix[:, t, :], op0=ALU.mult, op1=ALU.add).then_inc(s_res, 1)


def vit_layer(nc, dram, out):
    with ExitStack() as ctx:
        h = ctx.enter_context(nc.sbuf_tensor("h", [128, B, 2, D], F32))
        ident = ctx.enter_context(nc.sbuf_tensor("identity", [128, 128], F32))
        phase_one(nc, h, ident, dram)
        a1 = ctx.enter_context(nc.sbuf_tensor("a1", [HF + 1, 5, 2, FF], F32))
        a2 = ctx.enter_context(nc.sbuf_tensor("a2", [128, 5, FC, D], F32))
        s_experts = ctx.enter_context(nc.semaphore("s_experts"))
        phase_two(nc, h, ident, dram, out, a1, a2, s_experts)
        phase_three(nc, h, ident, dram, out, a1, a2, s_experts)


def rope_tables():
    inv = (np.float32(1.0) / np.float32(10000.0) ** (np.arange(0, HD, 2, dtype=np.float32) / np.float32(HD)))
    angle = np.arange(T, dtype=np.float32)[:, None] * inv.astype(np.float32)[None, :]
    cos, sin = np.cos(angle), np.sin(angle)
    return np.concatenate([cos, cos], 1), np.concatenate([-sin, sin], 1)


def by_tiles(rows):
    full = np.zeros((2 * T0, rows.shape[1]), rows.dtype)
    full[:T] = rows
    return np.ascontiguousarray(full.reshape(2, T0, -1).transpose(1, 0, 2))


def in_chunks(w, bias=None):
    full = np.zeros((HF + 1, 2, w.shape[0]), w.dtype)
    full[:HF] = w.T.reshape(2, HF, -1).transpose(1, 0, 2)
    if bias is not None:
        full[HF, 0] = bias
    return full


def kernel(**inputs):
    import concourse.bacc as bacc
    from concourse.bass_utils import run_bass_kernel_spmd

    a = {k: np.asarray(v) for k, v in inputs.items()}
    f32 = np.float32
    patches = a["x"].reshape(B, 3, 14, 16, 14, 16).transpose(0, 1, 3, 5, 2, 4).reshape(B, KC, 128, T - 2)
    x = np.zeros((B, 128, KC, T), f32)
    x[:, :, :, 2:] = patches.transpose(0, 2, 1, 3)
    embed_a = np.concatenate([a["cls_tok"][0], a["L0_tok_cls_token"][0],
                              np.broadcast_to(a["L0_tok_conv_b"], (T - 2, D))])
    embed_b = np.concatenate([np.zeros((1, D), f32), a["L0_tok_pos_emb"][0]])
    cos, sin = rope_tables()
    later = np.where(np.arange(T)[None, :] > np.arange(T)[:, None], f32(FAR), f32(0))
    wq, wk, wv = (a[f"L0_attn_W{n}"] for n in "qkv")
    bqkv = np.concatenate([a[f"L0_attn_b{n}"] for n in "qkv"])
    a1 = np.stack([in_chunks(a["L0_ffn_A1_W"][n].T, a["L0_ffn_A1_b"][n]) for n in range(5)], 1)
    e_b2 = np.zeros((2, 64, NCLS // 2, 2, D), f32)
    for i, e, (_, c) in COMBOS:
        e_b2[i % 2, :, i // 2, e] = a["L0_ffn_A2_b"][c]
    gw = a["L0_ffn_G_W"].transpose(1, 0, 2).reshape(2, HF, 2 * NCLS).transpose(1, 0, 2)
    arrays = {
        "x": x.reshape(B, 128, KC * T),
        "conv_w": a["L0_tok_conv_w"].reshape(D, KC, 128).transpose(2, 1, 0),
        "embed_a": by_tiles(embed_a), "embed_b": by_tiles(embed_b),
        "wqkv": in_chunks(np.concatenate([wq, wk, wv]), bqkv),
        "wo": in_chunks(a["L0_attn_Wo"], a["L0_attn_bo"]),
        "cos": by_tiles(cos), "sin": by_tiles(sin),
        "mask0": later[:T0, :T0], "mask1": later[T0:],
        "ident": np.eye(128, dtype=f32),
        "w1": in_chunks(a["L0_ffn_moe0_W1"].T, a["L0_ffn_moe0_b1"]),
        "w2": a["L0_ffn_moe0_W2"].reshape(FC, 128, D).transpose(1, 0, 2),
        "b2": np.broadcast_to(a["L0_ffn_moe0_b2"], (128, D)),
        "a1": a1, "a2": a["L0_ffn_A2_W"].reshape(5, FC, 128, D).transpose(2, 0, 1, 3),
        "gate_w": gw, "e_b2": e_b2.reshape(128, NCLS // 2, 2, D),
    }
    arrays = {f"in_{k}": np.ascontiguousarray(v) for k, v in arrays.items()}
    nc = bacc.Bacc("TRN2", target_bir_lowering=False, num_devices=1)
    dram = {k[3:]: nc.dram_tensor(k, v.shape, F32, kind="ExternalInput").ap() for k, v in arrays.items()}
    out = nc.dram_tensor("out", [B, T, D], F32, kind="ExternalOutput").ap()
    vit_layer(nc, dram, out)
    result = run_bass_kernel_spmd(nc, [arrays], core_ids=[0])
    return result.results[0]["out"]
```

```python
from contextlib import ExitStack

import numpy as np

import concourse.bass as bass
from concourse import mybir

F32 = mybir.dt.float32
F32R = mybir.dt.float32r
ALU = mybir.AluOpType
ACT = mybir.ActivationFunctionType

B = 64
D = 192
T = 198
T0, T1 = 128, T - 128
TILES = ((0, T0), (T0, T1))
KC = 6
H, HD = 12, 16
VC = 32
G = H // 4
PAIRS = H // 2
HF = D // 2
FF = 768
FC = FF // 128
UB = 3
NCLS = 6
NT = NCLS // 2
EPS = 1e-5
SCALE = HD ** -0.5
FAR = -1.0e30
TO_T = 3
VALUES_AT = {8: (0, 0), 0: (-1, 1), 4: (-1, 2)}
ON_ACT = (1, 5, 6, 8)
CONV_AT = (0, 2, 2, 4, 5, 7, 8, 11, 12, 12, 12, 12, 12)
PAIRS_NEXT = {9: 0, 10: 1, 11: 2}
PAIRS_THIS = {0: 3, 2: 4, 3: 5}
PAIR_BANK = (0, 1, 0, 1, 1, 1)
EMBED_AT, MOMENTS_AT, AGGREGATE_AT = 7, 8, 11
NORMALISE_AT, Z_AT, Z_HIGH_AT, Z_LOW_AT = 0, 1, 1, 2
QK_AT, ROTATE_AT, HIGH_AT = {3: 0, 5: 1}, {4: 0, 6: 1}, {5: 0, 7: 1}
V_AT, V_COPY_AT = 8, 8
O_AT, O_NORMAL_AT = {5: 0, 6: 1}, {5: 0, 6: 1}
ON_AT, ON_COPY_AT, WO_AT, RESIDUAL_AT = 7, 7, 9, 9

GROUPS = ((0, 3), (0, 4), (1, 3), (1, 4), (2, 3), (2, 4))
COMBOS = [(i, e, (a, c) if e == 0 else (c, a)) for i, (a, c) in enumerate(GROUPS) for e in range(2)]


def live(m):
    return not isinstance(m, int) or 0 <= m < B


def after(engine, sem, count, all_of_them=None):
    if isinstance(count, int):
        if count <= 0:
            return
        count = count if all_of_them is None else min(count, all_of_them)
    engine.wait_ge(sem, count)


def over_images(engine, steps):
    for i in (-2, -1, 0, 1):
        steps(i)
    with engine.Fori(2, B - 2) as i:
        steps(i)
    for i in (B - 2, B - 1, B):
        steps(i)


def phase_one(nc, h, ident, dram, next_weights, s_w):
    with ExitStack() as ctx:
        def sb(name, shape, dt=F32):
            return ctx.enter_context(nc.sbuf_tensor(name, shape, dt))

        def sem(name):
            return ctx.enter_context(nc.semaphore(name))

        conv_w = sb("conv_w", [128, KC, D])
        embed = sb("embed", [128, 2, D])
        wqkv_hi = sb("wqkv_hi", [HF + 1, 2, 3 * D], F32R)
        wqkv_lo = sb("wqkv_lo", [HF + 1, 2, 3 * D], F32R)
        wo = sb("wo", [HF + 1, 2, D])
        cos = sb("cos", [128, 2, HD])
        sin = sb("sin", [128, 2, HD])
        mask0 = sb("mask0", [128, T0])
        mask1 = sb("mask1", [T1, T])
        x = sb("x", [128, KC, T])
        stats = sb("stats", [128, 2, 6])
        mv = sb("mv", [128, 2, 2])
        veps = sb("veps", [128, 2])
        minus_half = sb("minus_half", [128, 2])
        eps = sb("eps", [128, 2])
        carrier = sb("carrier", [1, 16])
        zeros = sb("zeros", [128, 2, D])
        rstd = sb("rstd", [128, 2])
        z = sb("z", [128, 2, D])
        zT_hi = sb("zT_hi", [HF + 1, 2, T], F32R)
        zT_lo = sb("zT_lo", [HF + 1, 2, T], F32R)
        rope_c = sb("rope_c", [128, 2, 2 * D])
        rope_s = sb("rope_s", [128, 2, 2 * D])
        rope = sb("rope", [128, 2, 2 * D])
        parts = sb("parts", [128, 2, 2, H, 4, HD], F32R)
        partsT = sb("partsT", [128, PAIRS, 2, T], F32R)
        v_stage = sb("v_stage", [128, 2, D])
        v = sb("v", [128, 2, H, VC])
        masked = sb("masked", [128, 3, T0 + T])
        negmax = sb("negmax", [128, H, 2])
        probs = sb("probs", [128, 4, T0 + T])
        probsT = sb("probsT", [128, 6, T + T1])
        oT = sb("oT", [128, G, T])
        rowsum_inv = sb("rowsum_inv", [128, 2, H])
        o = sb("o", [128, 2, D])
        onT = sb("onT", [HF + 1, 2, T])

        wqkv = probsT[0:HF + 1, :, :].rearrange("p a b -> p (a b)")[:, 0:6 * D].rearrange("p (k f) -> p k f", k=2)
        embed_pos = probs[:, :, :].rearrange("p a b -> p (a b)")[:, 0:2 * D].rearrange("p (t d) -> p t d", t=2)

        ps = [ctx.enter_context(nc.psum_tensor(f"ps{i}", [128, 512], F32)) for i in range(8)]
        ps_a, ps_b, ps_o, ps_c = ps[0], ps[1], ps[2], ps[3]
        ps_s = ps[4:6]
        ps_p = ps[6:8]

        s_conv_w = sem("s_conv_w")
        s_const = sem("s_const")
        s_wqkv = sem("s_wqkv")
        s_preset = sem("s_preset")
        s_embed = sem("s_embed")
        s_x = sem("s_x")
        s_conv = sem("s_conv")
        s_h0 = sem("s_h0")
        s_stats = sem("s_stats")
        s_mv = sem("s_mv")
        s_veps = sem("s_veps")
        s_rstd = sem("s_rstd")
        s_z = sem("s_z")
        s_zT_ps = sem("s_zT_ps")
        s_zT_hi = sem("s_zT_hi")
        s_zT = sem("s_zT")
        s_qk = sem("s_qk")
        s_qk_read = sem("s_qk_read")
        s_rope = sem("s_rope")
        s_hi = sem("s_hi")
        s_parts = sem("s_parts")
        s_v_ps = sem("s_v_ps")
        s_v_stage = sem("s_v_stage")
        s_v = sem("s_v")
        s_partsT_ps = sem("s_partsT_ps")
        s_partsT = sem("s_partsT")
        s_scores = sem("s_scores")
        s_masked = sem("s_masked")
        s_probs = sem("s_probs")
        s_pT_ps = sem("s_pT_ps")
        s_pT = sem("s_pT")
        s_pT_act = sem("s_pT_act")
        s_pv = sem("s_pv")
        s_oT = sem("s_oT")
        s_o_ps = sem("s_o_ps")
        s_rsum = sem("s_rsum")
        s_o = sem("s_o")
        s_onT_ps = sem("s_onT_ps")
        s_onT = sem("s_onT")
        s_wo = sem("s_wo")
        s_h1 = sem("s_h1")

        consts = [(wqkv, dram["wqkv"]), (embed, dram["embed_a"]), (embed_pos, dram["embed_b"]),
                  (wo, dram["wo"]), (cos, dram["cos"]), (sin, dram["sin"]),
                  (mask0, dram["mask0"]), (mask1, dram["mask1"]), (ident, dram["ident"])]
        PRESETS = 20

        on_dve = tuple(k for k in range(H) if k not in ON_ACT)

        def copied(i, k):
            i, k = (i, k) if k >= 0 else (i - 1, k + H)
            sem_of, heads = (s_pT_act, ON_ACT) if k in ON_ACT else (s_pT, on_dve)
            return sem_of, i * len(heads) + heads.index(k) + 1

        def twice(t, w):
            n = TILES[t][1]
            return rope[0:n, t, w * D:(w + 1) * D].rearrange("p (h o d) -> p h o d", h=H, o=1)\
                .broadcast_to([n, H, 2, HD])

        def parts_of(t, w):
            blocks = parts[0:TILES[t][1], t, w, :, :, :]
            if w == 0:
                return blocks[:, :, 0:2, :], blocks[:, :, 2:4, :]
            return blocks[:, :, 0:4:2, :], blocks[:, :, 1:4:2, :]

        block = ctx.enter_context(nc.Block())

        @block.sync
        def _(sp):
            def load_x(m):
                after(sp, s_conv, m)
                sp.dma_start(x[:, :, :], dram["x"][bass.ds(m, 1)].rearrange("o p n -> p (o n)")
                             .rearrange("p (c t) -> p c t", c=KC)).then_inc(s_x, 16)

            sp.dma_start(conv_w[:], dram["conv_w"]).then_inc(s_conv_w, 16)
            load_x(0)
            for to, source in consts:
                sp.dma_start(to[:, :, :] if len(to.shape) == 3 else to[:, :], source).then_inc(s_const, 16)
            load_x(1)
            for to, source in zip(next_weights, ("w1", "w2", "b2")):
                sp.dma_start(to[:], dram[source]).then_inc(s_w, 16)
            with sp.Fori(2, B) as m:
                load_x(m)

        @block.gpsimd
        def _(pool):
            pool.memset(minus_half[:, :], -0.5).then_inc(s_preset, 1)
            pool.memset(eps[:, :], EPS).then_inc(s_preset, 1)
            pool.memset(mv[:, :, :], 1.0).then_inc(s_preset, 1)
            pool.memset(v[:, :, :, 0:HD], 0.0).then_inc(s_preset, 1)
            pool.memset(v[:, :, :, HD:HD + 1], 1.0).then_inc(s_preset, 1)
            pool.memset(v[:, :, :, HD + 1:VC], 0.0).then_inc(s_preset, 1)
            pool.memset(v_stage[:, :, :], 0.0).then_inc(s_preset, 1)
            pool.memset(zeros[:, :, :], 0.0).then_inc(s_preset, 1)
            pool.wait_ge(s_preset, PRESETS)

            def rstd_of(m):
                pool.wait_ge(s_mv, m * 2 + 2)
                after(pool, s_z, m * 2)
                pool.tensor_tensor(veps[:, :], mv[:, :, 1], eps[:, :], ALU.add).then_inc(s_veps, 1)
                pool.wait_ge(s_veps, m + 1)
                pool.tensor_tensor(rstd[:, :], veps[:, :], minus_half[:, :], ALU.pow).then_inc(s_rstd, 1)

            def low_parts(m, t):
                n = TILES[t][1]
                pool.wait_ge(s_qk_read, m * 2 + t + 1)
                after(pool, s_parts, m * 4 + 2 * t - 2)
                pool.tensor_tensor(rope[0:n, t, :], rope_c[0:n, t, :], rope_s[0:n, t, :], ALU.add)\
                    .then_inc(s_rope, 1)
                pool.wait_ge(s_hi, m * 4 + 2 * t + 2)
                for w in range(2):
                    hi, lo = parts_of(t, w)
                    pool.tensor_tensor(lo, twice(t, w), hi.bitcast(F32), ALU.subtract).then_inc(s_parts, 1)

            def spread_v(m, g):
                pool.wait_ge(s_v_stage, m * 2 + 2)
                after(pool, s_pv, m * G - G + g + 1)
                four = slice(4 * g * HD, 4 * (g + 1) * HD)
                pool.tensor_tensor(v[:, :, 4 * g:4 * g + 4, 0:HD],
                                   v_stage[:, :, four].rearrange("p t (h d) -> p t h d", h=4),
                                   zeros[:, :, four].rearrange("p t (h d) -> p t h d", h=4), ALU.add)\
                    .then_inc(s_v, 1)

            def steps(i):
                if live(i + 1):
                    low_parts(i + 1, 0)
                    low_parts(i + 1, 1)
                    spread_v(i + 1, 0)
                if live(i + 2):
                    rstd_of(i + 2)
                if live(i + 1):
                    spread_v(i + 1, 1)
                    spread_v(i + 1, 2)

            over_images(pool, steps)

        @block.tensor
        def _(pe):
            def conv(m, first, last):
                for n in range(first, last):
                    t, c = n // KC, n % KC
                    at, rows = TILES[t]
                    if n == 0:
                        pe.wait_ge(s_x, m * 16 + 16)
                        after(pe, s_h0, m * 2)
                    mm = pe.matmul(ps_c[0:rows, t * D:(t + 1) * D], x[:, c, at:at + rows], conv_w[:, c, :],
                                   start=(c == 0), stop=(c == KC - 1))
                if last == 2 * KC:
                    mm.then_inc(s_conv, 1)

            def z_transpose(m):
                if isinstance(m, int) and m == 0:
                    pe.wait_ge(s_const, 16 * len(consts))
                    pe.wait_ge(s_wqkv, 2)
                pe.wait_ge(s_z, m * 2 + 2)
                after(pe, s_partsT, m * PAIRS - 3)
                for t, (at, n) in enumerate(TILES):
                    for k in range(2):
                        mm = pe.transpose(ps_a[0:HF, k * T + at:k * T + at + n],
                                          z[0:n, t, k * HF:(k + 1) * HF], ident[0:n, 0:n])
                mm.then_inc(s_zT_ps, 1)

            def project(to, m, t, first, last):
                at, n = TILES[t]
                products = [(rows, k, zz, w) for rows, k in ((HF + 1, 0), (HF, 1))
                            for zz, w in ((zT_hi, wqkv_hi), (zT_hi, wqkv_lo), (zT_lo, wqkv_hi))]
                for e, (rows, k, zz, w) in enumerate(products):
                    mm = pe.matmul(to, zz[0:rows, k, at:at + n], w[0:rows, k, first:last],
                                   start=(e == 0), stop=(e == len(products) - 1))
                return mm

            def qk(m, t):
                n = TILES[t][1]
                if t == 0:
                    pe.wait_ge(s_zT, m + 1)
                else:
                    pe.wait_ge(s_qk_read, m * 2 + 1)
                project(ps_a[0:n, 0:2 * D], m, t, 0, 2 * D).then_inc(s_qk, 1)

            def values(m):
                pe.wait_ge(s_qk_read, m * 2 + 2)
                for t, (at, n) in enumerate(TILES):
                    mm = project(ps_a[0:n, t * D:(t + 1) * D], m, t, 2 * D, 3 * D)
                mm.then_inc(s_v_ps, 1)

            def parts_transpose(m, p):
                bank = (ps_a, ps_b)[PAIR_BANK[p]]
                if p == 0:
                    pe.wait_ge(s_parts, m * 4 + 4)
                    pe.wait_ge(s_v_stage, m * 2 + 2)
                elif p == 1:
                    after(pe, s_h1, m * 2 - 2, 2 * B)
                else:
                    pe.wait_ge(s_partsT, m * PAIRS + (p - 1 if p < 4 else p))
                for w in range(2):
                    for t, (at, n) in enumerate(TILES):
                        pair = parts[0:n, t, w, 2 * p:2 * p + 2, :, :].rearrange("p h b d -> p (h b d)")
                        mm = pe.transpose(bank[:, w * T + at:w * T + at + n], pair.bitcast(F32), ident[0:n, 0:n])
                mm.then_inc(s_partsT_ps, 1)

            def scores(i, k):
                p, r = k // 2, 64 * (k % 2)
                if k % 2 == 0:
                    pe.wait_ge(s_partsT, i * PAIRS + p + 1)
                after(pe, s_masked, i * H + k - 1)
                q, kk = partsT[r:r + 64, p, 0, :], partsT[r:r + 64, p, 1, :]
                bank = ps_s[k % 2]
                pe.matmul(bank[0:T0, 0:T0], q[:, 0:T0], kk[:, 0:T0], start=True, stop=True)
                pe.matmul(bank[0:T1, T0:T0 + T], q[:, T0:T], kk[:, 0:T], start=True, stop=True)\
                    .then_inc(s_scores, 1)

            def probs_transpose(i, k):
                if not (isinstance(i, int) and i == 0 and k < 2):
                    pe.wait_ge(*copied(i, k - 2))
                pe.wait_ge(s_probs, i * H + k + 1)
                bank, p = ps_p[k % 2], probs[:, k % 4, :]
                pe.transpose(bank[0:T0, 0:T0], p[0:T0, 0:T0], ident[:, :])
                pe.transpose(bank[0:T0, T0:T], p[0:T1, T0:2 * T0], ident[0:T1, 0:T1])
                pe.transpose(bank[0:T1, T:T + T1], p[0:T1, 2 * T0:T0 + T], ident[0:T1, 0:T1])\
                    .then_inc(s_pT_ps, 1)

            def values_of(b, g):
                last_dve = max(k for k in on_dve if k // 4 == g)
                last_act = max((k for k in ON_ACT if k // 4 == g), default=None)
                pe.wait_ge(*copied(b, last_dve))
                if last_act is not None:
                    pe.wait_ge(*copied(b, last_act))
                pe.wait_ge(s_v, b * G + g + 1)
                if g == 0:
                    after(pe, s_o, b * 2)
                else:
                    pe.wait_ge(s_oT, b * G + g)
                for rows, tile, columns, to in ((T0, 0, slice(0, T), slice(0, T)),
                                                (T1, 1, slice(T, T + T1), slice(T0, T))):
                    for r in range(4):
                        k = 4 * g + r
                        mm = pe.matmul(ps_o[32 * r:32 * r + 32, to], v[0:rows, tile, k, :],
                                       probsT[0:rows, k % 6, columns], start=(tile == 0), stop=(tile == 1),
                                       tile_position=(0, 32 * r))
                mm.then_inc(s_pv, 1)

            def o_transpose(b, t):
                at, n = TILES[t]
                if t == 0:
                    pe.wait_ge(s_oT, b * G + G)
                else:
                    pe.wait_ge(s_o, b * 2 + 1)
                for g in range(G):
                    mm = pe.transpose(ps_o[0:n, g * 128:(g + 1) * 128], oT[:, g, at:at + n], ident[:, :])
                mm.then_inc(s_o_ps, 1)

            def on_transpose(b):
                pe.wait_ge(s_o, b * 2 + 2)
                after(pe, s_partsT, b * PAIRS + 2 * PAIRS, B * PAIRS)
                after(pe, s_h1, b * 2)
                for t, (at, n) in enumerate(TILES):
                    for k in range(2):
                        mm = pe.transpose(ps_b[0:HF, k * T + at:k * T + at + n],
                                          o[0:n, t, k * HF:(k + 1) * HF], ident[0:n, 0:n])
                mm.then_inc(s_onT_ps, 1)

            def out_project(b):
                pe.wait_ge(s_onT, b + 1)
                for t, (at, n) in enumerate(TILES):
                    to = ps_b[0:n, t * D:(t + 1) * D]
                    pe.matmul(to, onT[:, 0, at:at + n], wo[:, 0, :], start=True, stop=False)
                    mm = pe.matmul(to, onT[0:HF, 1, at:at + n], wo[0:HF, 1, :], start=False, stop=True)
                mm.then_inc(s_wo, 1)

            def steps(i):
                for k in range(H):
                    if live(i):
                        scores(i, k)
                    j, kk = (i, k - TO_T) if k >= TO_T else (i - 1, k - TO_T + H)
                    if live(j):
                        probs_transpose(j, kk)
                    if k in VALUES_AT and live(i + VALUES_AT[k][0]):
                        values_of(i + VALUES_AT[k][0], VALUES_AT[k][1])
                    if live(i - 1):
                        if k in O_AT:
                            o_transpose(i - 1, O_AT[k])
                        if k == ON_AT:
                            on_transpose(i - 1)
                        if k == WO_AT:
                            out_project(i - 1)
                    if live(i + 2) and CONV_AT[k] < CONV_AT[k + 1]:
                        conv(i + 2, CONV_AT[k], CONV_AT[k + 1])
                    if live(i + 1):
                        if k == Z_AT:
                            z_transpose(i + 1)
                        if k in QK_AT:
                            qk(i + 1, QK_AT[k])
                        if k == V_AT:
                            values(i + 1)
                    if k in PAIRS_THIS and live(i):
                        parts_transpose(i, PAIRS_THIS[k])
                    if k in PAIRS_NEXT and live(i + 1):
                        parts_transpose(i + 1, PAIRS_NEXT[k])

            pe.wait_ge(s_conv_w, 16)
            pe.wait_ge(s_preset, PRESETS)
            over_images(pe, steps)

        @block.scalar
        def _(act):
            act.wait_ge(s_preset, PRESETS)

            def exps(i, k):
                act.wait_ge(s_masked, i * H + k + 1)
                after(act, s_pT_ps, i * H + k - 3)
                act.activation(probs[0:T0, k % 4, 0:T0], masked[0:T0, k % 3, 0:T0], ACT.Exp,
                               bias=negmax[0:T0, k, 0:1], scale=-1.0)
                act.activation(probs[0:T1, k % 4, T0:T0 + T], masked[0:T1, k % 3, T0:T0 + T], ACT.Exp,
                               bias=negmax[0:T1, k, 1:2], scale=-1.0).then_inc(s_probs, 1)

            def probs_copy(i, k):
                act.wait_ge(s_pT_ps, i * H + k + 1)
                act.activation(probsT[:, k % 6, :], ps_p[k % 2][:, 0:T + T1], ACT.Copy).then_inc(s_pT_act, 1)

            def z_high(m):
                act.wait_ge(s_zT_ps, m + 1)
                after(act, s_v_ps, m)
                act.activation(zT_hi[0:HF, :, :], ps_a[0:HF, 0:2 * T].rearrange("p (k t) -> p k t", k=2), ACT.Copy)\
                    .then_inc(s_zT_hi, 1)

            def o_copy(b, g):
                act.wait_ge(s_pv, b * G + g + 1)
                after(act, s_o_ps, b * 2)
                act.activation(oT[:, g, :], ps_o[:, 0:T], ACT.Copy).then_inc(s_oT, 1)

            def on_copy(b):
                act.wait_ge(s_onT_ps, b + 1)
                after(act, s_wo, b)
                act.activation(onT[0:HF, :, :], ps_b[0:HF, 0:2 * T].rearrange("p (k t) -> p k t", k=2), ACT.Copy)\
                    .then_inc(s_onT, 1)

            def v_copy(m):
                act.wait_ge(s_v_ps, m + 1)
                after(act, s_v, m * 3)
                for t, (at, n) in enumerate(TILES):
                    act.activation(v_stage[0:n, t, :], ps_a[0:n, t * D:(t + 1) * D], ACT.Copy)\
                        .then_inc(s_v_stage, 1)

            def parts_copy(m, p):
                act.wait_ge(s_partsT_ps, m * PAIRS + p + 1)
                after(act, s_scores, m * H - H + 2 * p + 2)
                bank = (ps_a, ps_b)[PAIR_BANK[p]]
                act.activation(partsT[:, p, :, :], bank[:, 0:2 * T].rearrange("p (w t) -> p w t", w=2), ACT.Copy)\
                    .then_inc(s_partsT, 1)

            def high_parts(m, t):
                n = TILES[t][1]
                act.wait_ge(s_rope, m * 2 + t + 1)
                after(act, s_partsT_ps, m * PAIRS)
                for w in range(2):
                    act.activation(parts_of(t, w)[0], twice(t, w), ACT.Copy).then_inc(s_hi, 1)

            def steps(i):
                for k in range(H):
                    if live(i - 1):
                        if k == ON_COPY_AT:
                            on_copy(i - 1)
                    j, kk = (i, k - TO_T) if k >= TO_T else (i - 1, k - TO_T + H)
                    if live(j) and kk in ON_ACT:
                        probs_copy(j, kk)
                    if live(i):
                        exps(i, k)
                    if k in VALUES_AT and live(i + VALUES_AT[k][0]):
                        o_copy(i + VALUES_AT[k][0], VALUES_AT[k][1])
                    if k in PAIRS_THIS and live(i):
                        parts_copy(i, PAIRS_THIS[k])
                    if live(i + 1):
                        if k == Z_HIGH_AT:
                            z_high(i + 1)
                        if k in HIGH_AT:
                            high_parts(i + 1, HIGH_AT[k])
                        if k == V_COPY_AT:
                            v_copy(i + 1)
                        if k in PAIRS_NEXT:
                            parts_copy(i + 1, PAIRS_NEXT[k])

            act.wait_ge(s_const, 16 * len(consts))
            act.activation(wqkv_hi[:, :, :], wqkv, ACT.Copy).then_inc(s_wqkv, 1)
            over_images(act, steps)

        @block.vector
        def _(dve):
            dve.memset(zT_hi[HF:HF + 1, :, :].bitcast(F32), 1.0).then_inc(s_preset, 1)
            dve.memset(zT_lo[HF:HF + 1, :, :].bitcast(F32), 0.0).then_inc(s_preset, 1)
            dve.memset(onT[HF:HF + 1, :, :], 1.0).then_inc(s_preset, 1)
            for bank in ps:
                dve.memset(bank[:, :], 0.0).then_inc(s_preset, 1)
            dve.wait_ge(s_const, 16 * len(consts))
            dve.tensor_tensor(embed[:, :, :], embed[:, :, :], embed_pos[:, :, :], ALU.add).then_inc(s_preset, 1)
            dve.wait_ge(s_preset, PRESETS)

            def probs_copy(i, k):
                dve.wait_ge(s_pT_ps, i * H + k + 1)
                dve.tensor_copy(probsT[:, k % 6, :], ps_p[k % 2][:, 0:T + T1]).then_inc(s_pT, 1)

            def row_max(i, k):
                after(dve, s_probs, i * H + k - 2)
                dve.wait_ge(s_scores, i * H + k + 1)
                dve.memset(carrier[:, k:k + 1], 0.0)
                bank = ps_s[k % 2]
                dve.tensor_tensor_reduce(masked[0:T0, k % 3, 0:T0], bank[0:T0, 0:T0], mask0[:, :], -SCALE, 1e38,
                                         ALU.add, ALU.min, negmax[0:T0, k, 0:1])
                dve.tensor_tensor_reduce(masked[0:T1, k % 3, T0:T0 + T], bank[0:T1, T0:T0 + T], mask1[:, :], -SCALE,
                                         1e38, ALU.add, ALU.min, negmax[0:T1, k, 1:2]).then_inc(s_masked, 1)

            def h_tile(m, t, n):
                return h[0:n, bass.ds(m, 1), t, :].rearrange("p o d -> p (o d)")

            def embed_add(m):
                dve.wait_ge(s_conv, m + 1)
                for t, (at, n) in enumerate(TILES):
                    dve.tensor_tensor(h_tile(m, t, n), ps_c[0:n, t * D:(t + 1) * D], embed[0:n, t, :], ALU.add)\
                        .then_inc(s_h0, 1)

            def moments(m):
                dve.wait_ge(s_h0, m * 2 + 2)
                dve.memset(carrier[:, 12:13], 0.0)
                for t, (at, n) in enumerate(TILES):
                    dve.bn_stats(stats[0:n, t, :], h_tile(m, t, n)).then_inc(s_stats, 1)

            def aggregate(m):
                dve.wait_ge(s_stats, m * 2 + 2)
                after(dve, s_rstd, m)
                dve.memset(carrier[:, 13:14], 0.0)
                for t, (at, n) in enumerate(TILES):
                    dve.bn_aggr(mv[0:n, t, :], stats[0:n, t, :]).then_inc(s_mv, 1)

            def normalise(m):
                dve.wait_ge(s_rstd, m + 1)
                after(dve, s_zT_ps, m)
                for t, (at, n) in enumerate(TILES):
                    dve.tensor_scalar(z[0:n, t, :], h_tile(m, t, n), mv[0:n, t, 0:1], rstd[0:n, t:t + 1],
                                      ALU.subtract, ALU.mult).then_inc(s_z, 1)

            def z_low(m):
                dve.wait_ge(s_zT_hi, m + 1)
                dve.tensor_tensor(zT_lo[0:HF, :, :], ps_a[0:HF, 0:2 * T].rearrange("p (k t) -> p k t", k=2),
                                  zT_hi[0:HF, :, :].bitcast(F32), ALU.subtract).then_inc(s_zT, 1)

            def rotate(m, t):
                n = TILES[t][1]
                dve.wait_ge(s_qk, m * 2 + t + 1)
                after(dve, s_parts, m * 4 + 2 * t - 2)
                heads = ps_a[0:n, 0:2 * D].rearrange("p (h d) -> p h d", d=HD)
                to_c = rope_c[0:n, t, :].rearrange("p (h d) -> p h d", d=HD)
                to_s = rope_s[0:n, t, :].rearrange("p (h d) -> p h d", d=HD)
                half = HD // 2

                def table(which, a, b):
                    return which[0:n, t, a:b].rearrange("p (o d) -> p o d", o=1).broadcast_to([n, 2 * H, b - a])

                dve.tensor_tensor(to_c, heads, table(cos, 0, HD), ALU.mult)
                dve.tensor_tensor(to_s[:, :, 0:half], heads[:, :, half:HD], table(sin, 0, half), ALU.mult)
                dve.tensor_tensor(to_s[:, :, half:HD], heads[:, :, 0:half], table(sin, half, HD), ALU.mult)\
                    .then_inc(s_qk_read, 1)

            def o_normalise(b, t):
                n = TILES[t][1]
                dve.wait_ge(s_o_ps, b * 2 + t + 1)
                heads = ps_o[0:n, 0:H * VC].rearrange("p (h d) -> p h d", d=VC)
                dve.reciprocal(rowsum_inv[0:n, t, :], heads[:, :, HD]).then_inc(s_rsum, 1)
                dve.wait_ge(s_rsum, b * 2 + t + 1)
                after(dve, s_onT_ps, b)
                dve.tensor_tensor(o[0:n, t, :].rearrange("p (h d) -> p h d", d=HD), heads[:, :, 0:HD],
                                  rowsum_inv[0:n, t, :].rearrange("p (h o) -> p h o", o=1)
                                  .broadcast_to([n, H, HD]), ALU.mult).then_inc(s_o, 1)

            def residual(b):
                dve.wait_ge(s_wo, b + 1)
                for t, (at, n) in enumerate(TILES):
                    dve.tensor_tensor(h_tile(b, t, n), h_tile(b, t, n), ps_b[0:n, t * D:(t + 1) * D], ALU.add)\
                        .then_inc(s_h1, 1)

            def steps(i):
                for k in range(H):
                    if live(i):
                        row_max(i, k)
                    j, kk = (i, k - TO_T) if k >= TO_T else (i - 1, k - TO_T + H)
                    if live(j) and kk in on_dve:
                        probs_copy(j, kk)
                    if live(i - 1):
                        if k in O_NORMAL_AT:
                            o_normalise(i - 1, O_NORMAL_AT[k])
                        if k == RESIDUAL_AT:
                            residual(i - 1)
                    if live(i + 2):
                        if k == EMBED_AT:
                            embed_add(i + 2)
                        if k == MOMENTS_AT:
                            moments(i + 2)
                        if k == AGGREGATE_AT:
                            aggregate(i + 2)
                    if live(i + 1):
                        if k == NORMALISE_AT:
                            normalise(i + 1)
                        if k == Z_LOW_AT:
                            z_low(i + 1)
                        if k in ROTATE_AT:
                            rotate(i + 1, ROTATE_AT[k])

            dve.wait_ge(s_wqkv, 1)
            dve.tensor_tensor(wqkv_lo[:, :, :], wqkv, wqkv_hi[:, :, :].bitcast(F32), ALU.subtract).then_inc(s_wqkv, 1)
            over_images(dve, steps)


def phase_two(nc, h, ident, dram, out, weights, s_w, experts, s_experts):
    with ExitStack() as ctx:
        def sb(name, shape, dt=F32):
            return ctx.enter_context(nc.sbuf_tensor(name, shape, dt))

        def sem(name):
            return ctx.enter_context(nc.semaphore(name))

        w1, w2, b2 = weights
        w1_hi = sb("w1_hi", [HF + 1, 2, FF], F32R)
        w1_lo = sb("w1_lo", [HF + 1, 2, FF], F32R)
        w2_parts = sb("w2_parts", [128, FC, 2, D], F32R)
        stats = sb("f_stats", [128, 2, 6])
        mv = sb("f_mv", [128, 2, 2])
        veps = sb("f_veps", [128, 2])
        minus_half = sb("f_minus_half", [128, 2])
        eps = sb("f_eps", [128, 2])
        carrier = sb("f_carrier", [1, 2])
        rstd = sb("f_rstd", [128, 2])
        z = sb("f_z", [128, 2, D])
        zT_hi = sb("f_zT_hi", [HF + 1, 2, 2 * T], F32R)
        zT_lo = sb("f_zT_lo", [HF + 1, 2, 2 * T], F32R)
        hidden = sb("hidden", [128, UB, 2 * T])
        hidden_hi = sb("hidden_hi", [128, FC, 2 * T], F32R)
        hidden_lo = sb("hidden_lo", [128, FC, 2 * T], F32R)
        result = sb("result", [128, 2, D])

        ps = [ctx.enter_context(nc.psum_tensor(f"f_ps{i}", [128, 512], F32)) for i in range(8)]
        ps_up, ps_z, ps_down = ps[0:UB], ps[3], ps[4:8]

        s_preset = sem("f_preset")
        s_w_hi = sem("f_w_hi")
        s_w_lo = sem("f_w_lo")
        s_stats = sem("f_stats_done")
        s_mv = sem("f_mv_done")
        s_veps = sem("f_veps_done")
        s_rstd = sem("f_rstd_done")
        s_z = sem("f_z_done")
        s_zT_ps = sem("f_zT_ps")
        s_zT_hi = sem("f_zT_hi_done")
        s_zT = sem("f_zT_done")
        s_up = sem("f_up")
        s_gelu = sem("f_gelu")
        s_hi = sem("f_hi")
        s_lo = sem("f_lo")
        s_down = sem("f_down")
        s_sum = sem("f_sum")
        s_result = sem("f_result")
        s_stored = sem("f_stored")

        PRESETS = 5
        block = ctx.enter_context(nc.Block())

        def over(engine, steps):
            for p in (-3, -2, -1, 0):
                steps(p)
            with engine.Fori(1, B // 2 - 3) as p:
                steps(p)
            for p in (B // 2 - 3, B // 2 - 2, B // 2 - 1):
                steps(p)

        def pair_live(p):
            return live(p) and live(p * 2)

        @block.sync
        def _(sp):
            a1, gate_w, e_b2, hc = experts
            for i in range(NCLS):
                r = 64 * (i % 2)
                sp.dma_start(hc[r:r + B, i // 2, :], h[i:i + 1, :, 0, :]).then_inc(s_experts, 16)
            for to, source in ((gate_w, dram["gate_w"]), (e_b2, dram["e_b2"]), (a1, dram["a1"][:, 0:NT])):
                sp.dma_start(to[:], source).then_inc(s_experts, 16)
            with sp.Fori(0, B) as j:
                sp.wait_ge(s_result, j * 2 + 1)
                sp.dma_start(out[bass.ds(j, 1), NCLS:T0, :].rearrange("o p d -> p (o d)"), result[NCLS:T0, 0, :])\
                    .then_inc(s_stored, 16)
                sp.wait_ge(s_result, j * 2 + 2)
                sp.dma_start(out[bass.ds(j, 1), T0:T, :].rearrange("o p d -> p (o d)"), result[0:T1, 1, :])\
                    .then_inc(s_stored, 16)
            sp.wait_ge(s_stored, 32 * B)

        def h_tile(m, t, n):
            return h[0:n, bass.ds(m, 1), t, :].rearrange("p o d -> p (o d)")

        @block.gpsimd
        def _(pool):
            pool.memset(minus_half[:, :], -0.5).then_inc(s_preset, 1)
            pool.memset(eps[:, :], EPS).then_inc(s_preset, 1)
            pool.memset(mv[:, :, :], 1.0).then_inc(s_preset, 1)
            pool.wait_ge(s_preset, PRESETS)

            def rstd_of(m):
                pool.wait_ge(s_mv, m * 2 + 2)
                after(pool, s_z, m * 2)
                pool.tensor_tensor(veps[:, :], mv[:, :, 1], eps[:, :], ALU.add).then_inc(s_veps, 1)
                pool.wait_ge(s_veps, m + 1)
                pool.tensor_tensor(rstd[:, :], veps[:, :], minus_half[:, :], ALU.pow).then_inc(s_rstd, 1)

            def low(p, c):
                pool.wait_ge(s_hi, p * FC + c + 1)
                pool.tensor_tensor(hidden_lo[:, c, :], hidden[:, c % UB, :], hidden_hi[:, c, :].bitcast(F32),
                                   ALU.subtract).then_inc(s_lo, 1)

            def steps(p):
                for q in range(2):
                    m = p * 2 + 6 + q
                    if live(m):
                        rstd_of(m)
                    if pair_live(p + 1):
                        for c in range(UB * q, UB * (q + 1)):
                            low(p + 1, c)

            over(pool, steps)

        @block.tensor
        def _(pe):
            pe.wait_ge(s_preset, PRESETS)

            def transpose_z(m):
                pe.wait_ge(s_z, m * 2 + 2)
                after(pe, s_zT, m)
                for t, (at, n) in enumerate(TILES):
                    for k in range(2):
                        mm = pe.transpose(ps_z[0:HF, k * T + at:k * T + at + n],
                                          z[0:n, t, k * HF:(k + 1) * HF], ident[0:n, 0:n])
                mm.then_inc(s_zT_ps, 1)

            def up(p):
                pe.wait_ge(s_zT, p * 2 + 2)
                for c in range(FC):
                    after(pe, s_gelu, p * FC + c + 1 - UB)
                    products = [(rows, k, w, zz) for rows, k in ((HF + 1, 0), (HF, 1))
                                for w, zz in ((w1_hi, zT_hi), (w1_hi, zT_lo), (w1_lo, zT_hi))]
                    for e, (rows, k, w, zz) in enumerate(products):
                        mm = pe.matmul(ps_up[c % UB][:, 0:2 * T], w[0:rows, k, c * 128:(c + 1) * 128],
                                       zz[0:rows, k, :], start=(e == 0), stop=(e == len(products) - 1))
                    mm.then_inc(s_up, 1)

            def down(p, first, last):
                if first == 0:
                    after(pe, s_result, p * 4)
                for c in range(first, last):
                    pe.wait_ge(s_lo, p * FC + c + 1)
                    for q in range(2):
                        for t, (at, n) in enumerate(TILES):
                            rows = slice(q * T + at, q * T + at + n)
                            wide = (ps_down[2 * q + t][0:n, 0:2 * D], hidden_hi[:, c, rows],
                                    w2_parts[:, c, :, :].rearrange("p e d -> p (e d)"))
                            narrow = (ps_down[2 * q + t][0:n, 0:D], hidden_lo[:, c, rows], w2_parts[:, c, 0, :])
                            for operands in ((narrow, wide) if c == FC - 1 else (wide, narrow)):
                                mm = pe.matmul(*operands, start=(c == 0 and operands is wide),
                                               stop=(c == FC - 1 and operands is wide))
                    mm.then_inc(s_down, 1)

            def steps(p):
                if pair_live(p + 1):
                    up(p + 1)
                for q in range(2):
                    if pair_live(p + 2):
                        transpose_z(p * 2 + 4 + q)
                    if pair_live(p):
                        down(p, UB * q, UB * (q + 1))

            pe.wait_ge(s_w_lo, 2)
            over(pe, steps)

        @block.scalar
        def _(act):
            act.wait_ge(s_w, 16 * 3)
            act.activation(w1_hi[:, :, :], w1[:, :, :], ACT.Copy).then_inc(s_w_hi, 1)
            act.activation(w2_parts[:, :, 0, :], w2[:, :, :], ACT.Copy).then_inc(s_w_hi, 1)
            act.wait_ge(s_preset, PRESETS)

            def z_high(m, q):
                act.wait_ge(s_zT_ps, m + 1)
                after(act, s_up, (m - q) * (FC // 2))
                act.activation(zT_hi[0:HF, :, q * T:(q + 1) * T], ps_z[0:HF, 0:2 * T]
                               .rearrange("p (k t) -> p k t", k=2), ACT.Copy).then_inc(s_zT_hi, 1)

            def gelu(p, c):
                act.wait_ge(s_up, p * FC + c + 1)
                after(act, s_lo, p * FC + c + 1 - UB)
                act.activation(hidden[:, c % UB, :], ps_up[c % UB][:, 0:2 * T], ACT.Gelu).then_inc(s_gelu, 1)

            def steps(p):
                for c in range(FC):
                    if pair_live(p + 1):
                        gelu(p + 1, c)
                    if c == UB - 1 and pair_live(p + 2):
                        z_high(p * 2 + 4, 0)
                        z_high(p * 2 + 5, 1)

            over(act, steps)

        @block.vector
        def _(dve):
            dve.memset(zT_hi[HF:HF + 1, :, :].bitcast(F32), 1.0).then_inc(s_preset, 1)
            dve.memset(zT_lo[HF:HF + 1, :, :].bitcast(F32), 0.0).then_inc(s_preset, 1)

            def moments(m):
                for t, (at, n) in enumerate(TILES):
                    dve.bn_stats(stats[0:n, t, :], h_tile(m, t, n)).then_inc(s_stats, 1)
                after(dve, s_rstd, m)
                dve.wait_ge(s_stats, m * 2 + 2)
                dve.memset(carrier[:, 0:1], 0.0)
                for t, (at, n) in enumerate(TILES):
                    dve.bn_aggr(mv[0:n, t, :], stats[0:n, t, :]).then_inc(s_mv, 1)

            def normalise(m):
                dve.wait_ge(s_rstd, m + 1)
                after(dve, s_zT_ps, m)
                for t, (at, n) in enumerate(TILES):
                    dve.tensor_scalar(z[0:n, t, :], h_tile(m, t, n), mv[0:n, t, 0:1], rstd[0:n, t:t + 1],
                                      ALU.subtract, ALU.mult).then_inc(s_z, 1)

            def z_low(m, q):
                dve.wait_ge(s_zT_hi, m + 1)
                dve.tensor_tensor(zT_lo[0:HF, :, q * T:(q + 1) * T], ps_z[0:HF, 0:2 * T]
                                  .rearrange("p (k t) -> p k t", k=2),
                                  zT_hi[0:HF, :, q * T:(q + 1) * T].bitcast(F32), ALU.subtract).then_inc(s_zT, 1)

            def high(p, c):
                dve.wait_ge(s_gelu, p * FC + c + 1)
                after(dve, s_down, p * FC - FC + c + 1)
                dve.tensor_copy(hidden_hi[:, c, :], hidden[:, c % UB, :]).then_inc(s_hi, 1)

            def finish(m, p, q):
                def add(t, a, b):
                    return dve.tensor_tensor(result[0:TILES[t][1], t, :], a, b, ALU.add)

                for t, (at, n) in enumerate(TILES):
                    dve.wait_ge(s_down, p * FC + FC)
                    after(dve, s_stored, m * 32)
                    add(t, ps_down[2 * q + t][0:n, 0:D], b2[0:n, :]).then_inc(s_sum, 1)
                for t, (at, n) in enumerate(TILES):
                    dve.wait_ge(s_sum, m * 4 + t + 1)
                    add(t, result[0:n, t, :], h_tile(m, t, n)).then_inc(s_sum, 1)
                for t, (at, n) in enumerate(TILES):
                    dve.wait_ge(s_sum, m * 4 + t + 3)
                    add(t, result[0:n, t, :], ps_down[2 * q + t][0:n, D:2 * D]).then_inc(s_result, 1)

            def steps(p):
                for q in range(2):
                    m = p * 2 + 4 + q
                    if pair_live(p + 2):
                        z_low(m, q)
                    if live(m + 1):
                        normalise(m + 1)
                    if live(m + 2):
                        moments(m + 2)
                    if pair_live(p + 1):
                        for c in range(UB * q, UB * (q + 1)):
                            high(p + 1, c)
                if pair_live(p):
                    finish(p * 2, p, 0)
                    finish(p * 2 + 1, p, 1)

            dve.wait_ge(s_preset, PRESETS)
            for n, (w, hi, lo) in enumerate(((w1, w1_hi[:, :, :], w1_lo[:, :, :]),
                                             (w2, w2_parts[:, :, 0, :], w2_parts[:, :, 1, :]))):
                dve.wait_ge(s_w_hi, n + 1)
                dve.tensor_tensor(lo, w[:, :, :], hi.bitcast(F32), ALU.subtract).then_inc(s_w_lo, 1)
            over(dve, steps)


def phase_three(nc, ident, dram, out, experts, s_experts):
    WIDE = [128] * NT + [64 * NT] * 2

    with ExitStack() as ctx:
        def sb(name, shape, dt=F32):
            return ctx.enter_context(nc.sbuf_tensor(name, shape, dt))

        def sem(name):
            return ctx.enter_context(nc.semaphore(name))

        a1_rest = sb("a1_rest", [HF + 1, 2, 2, FF])
        a2 = sb("a2", [128, 5, FC, D])
        a1, gate_w, b2, hc = experts
        stats = sb("e_stats", [128, NT, 6])
        mv = sb("e_mv", [128, NT, 2])
        veps = sb("e_veps", [128, NT])
        minus_half = sb("e_minus_half", [128, NT])
        rstd = sb("e_rstd", [128, NT])
        z = sb("e_z", [128, NT, D])
        zT = sb("e_zT", [HF + 1, 2, NT * 128])
        hidden = sb("e_hidden", [128, FC, 2 * NT * 128])
        logits = sb("logits", [128, NT, 2])
        top = sb("top", [128, NT])
        shifted = sb("shifted", [128, NT, 2])
        expd = sb("expd", [128, NT, 2])
        total = sb("total", [128, NT])
        total_inv = sb("total_inv", [128, NT])
        gate = sb("gate", [128, NT, 2])
        least = sb("least", [128, NT])
        above = sb("above", [128, NT, 2])
        kept = sb("kept", [128, NT, 2])
        kept_sum = sb("kept_sum", [128, NT])
        kept_clip = sb("kept_clip", [128, NT])
        kept_inv = sb("kept_inv", [128, NT])
        share = sb("share", [128, NT, 2])
        y = sb("e_y", [128, NT, 2, D])
        mix = sb("e_mix", [128, NT, D])
        res = sb("e_res", [128, NT, D])

        ps = [ctx.enter_context(nc.psum_tensor(f"e_ps{i}", [128, 512], F32)) for i in range(8)]
        ps_z, ps_gate, ps_up, ps_y = ps[0:2], ps[2], ps[3:5], ps[5:8]

        s_a1 = sem("e_a1")
        s_a2 = sem("e_a2")
        s_preset = sem("e_preset")
        s_stats = sem("e_stats_done")
        s_mv = sem("e_mv_done")
        s_rstd = sem("e_rstd_done")
        s_z = sem("e_z_done")
        s_zT_ps = sem("e_zT_ps")
        s_zT = sem("e_zT_done")
        s_gate_ps = sem("e_gate_ps")
        s_shift = sem("e_shift")
        s_exp = sem("e_exp")
        s_share = sem("e_share")
        s_up = sem("e_up")
        s_gelu = sem("e_gelu")
        s_y = sem("e_y_ps")
        s_yb = sem("e_yb")
        s_mix = sem("e_mix_done")
        s_res = sem("e_res_done")
        s_out = sem("e_out")

        PRESETS = 2
        block = ctx.enter_context(nc.Block())

        @block.sync
        def _(sp):
            sp.dma_start(a1_rest[:], dram["a1"][:, NT:]).then_inc(s_a1, 16)
            sp.dma_start(a2[:], dram["a2"]).then_inc(s_a2, 16)
            sp.wait_ge(s_res, NT)
            for i in range(NCLS):
                r = 64 * (i % 2)
                sp.dma_start(out[:, i, :], res[r:r + B, i // 2, :]).then_inc(s_out, 16)
            sp.wait_ge(s_out, 16 * NCLS)

        @block.gpsimd
        def _(pool):
            pool.memset(minus_half[:, :], -0.5).then_inc(s_preset, 1)
            pool.wait_ge(s_preset, PRESETS)
            pool.wait_ge(s_mv, NT)
            pool.tensor_scalar(veps[:, :], mv[:, :, 1], EPS, None, ALU.add).then_inc(s_rstd, 1)
            pool.wait_ge(s_rstd, 1)
            pool.tensor_tensor(rstd[:, :], veps[:, :], minus_half[:, :], ALU.pow).then_inc(s_rstd, 1)

        def tokens(a):
            if a < NT:
                return lambda part, k: zT[0:part, k, a * 128:(a + 1) * 128]
            return lambda part, k: zT[0:part, k, :].rearrange("p (t q b) -> p t q b", t=NT, q=2)[:, :, a - NT, :]

        @block.tensor
        def _(pe):
            pe.wait_ge(s_preset, PRESETS)
            pe.wait_ge(s_z, NT)
            for k in range(2):
                for t in range(NT):
                    mm = pe.transpose(ps_z[k][0:HF, t * 128:(t + 1) * 128], z[:, t, k * HF:(k + 1) * HF], ident[:, :])
            mm.then_inc(s_zT_ps, 1)
            pe.wait_ge(s_zT, 2)
            pe.wait_ge(s_experts, 16 * (NCLS + 3))
            for t in range(NT):
                for k in range(2):
                    mm = pe.matmul(ps_gate[:, 4 * t:4 * t + 4], zT[0:HF, k, t * 128:(t + 1) * 128],
                                   gate_w[:, k, 4 * t:4 * t + 4], start=(k == 0), stop=(k == 1))
            mm.then_inc(s_gate_ps, 1)
            n = 0
            for a in range(5):
                wide = WIDE[a]
                first_layer = a1[:, a] if a < NT else a1_rest[:, a - NT]
                if a == NT:
                    pe.wait_ge(s_a1, 16)
                for u in range(FC // 2):
                    if n >= 2:
                        pe.wait_ge(s_gelu, n - 1)
                    for c in (2 * u, 2 * u + 1):
                        to = ps_up[n % 2][:, (c % 2) * wide:(c % 2 + 1) * wide]
                        pe.matmul(to, first_layer[:, 0, c * 128:(c + 1) * 128], tokens(a)(HF + 1, 0),
                                  start=True, stop=False)
                        mm = pe.matmul(to, first_layer[0:HF, 1, c * 128:(c + 1) * 128], tokens(a)(HF, 1),
                                       start=False, stop=True)
                    mm.then_inc(s_up, 1)
                    n += 1
            pe.wait_ge(s_gelu, n)
            pe.wait_ge(s_a2, 16)
            for t in range(NT):
                for q in range(2):
                    for c in range(FC):
                        mm = pe.matmul(ps_y[t][64 * q:64 * q + 64, 0:D], hidden[:, c, 128 * t + 64 * q:128 * t + 64 * q + 64],
                                       a2[:, NT + q, c, :], start=(c == 0), stop=(c == FC - 1),
                                       tile_position=(0, 64 * q))
                mm.then_inc(s_y, 1)
                for c in range(FC):
                    second = hidden[:, c, (NT + t) * 128:(NT + t + 1) * 128]
                    mm = pe.matmul(ps_y[t][:, D:2 * D], second, a2[:, t, c, :], start=(c == 0), stop=(c == FC - 1))
                mm.then_inc(s_y, 1)

        @block.scalar
        def _(act):
            act.wait_ge(s_preset, PRESETS)
            act.wait_ge(s_zT_ps, 1)
            for k in range(2):
                act.activation(zT[0:HF, k, :], ps_z[k][0:HF, 0:NT * 128], ACT.Copy).then_inc(s_zT, 1)
            act.wait_ge(s_shift, 1)
            act.activation(expd[:, :, :], shifted[:, :, :], ACT.Exp).then_inc(s_exp, 1)
            n = 0
            for a in range(5):
                wide = WIDE[a]
                for u in range(FC // 2):
                    act.wait_ge(s_up, n + 1)
                    if a < NT:
                        to = hidden[:, 2 * u:2 * u + 2, 128 * a:128 * a + 128]
                        source = ps_up[n % 2][:, 0:2 * wide].rearrange("p (c t) -> p c t", c=2)
                    else:
                        to = hidden[:, 2 * u:2 * u + 2, 128 * NT:].rearrange("p c (t q b) -> p c t q b", t=NT, q=2)\
                            [:, :, :, a - NT, :]
                        source = ps_up[n % 2][:, 0:2 * wide].rearrange("p (c t b) -> p c t b", c=2, t=NT)
                    act.activation(to, source, ACT.Gelu).then_inc(s_gelu, 1)
                    n += 1

        @block.vector
        def _(dve):
            dve.memset(zT[HF:HF + 1, 0, :], 1.0).then_inc(s_preset, 1)
            dve.wait_ge(s_experts, 16 * (NCLS + 3))
            for t in range(NT):
                dve.bn_stats(stats[:, t, :], hc[:, t, :]).then_inc(s_stats, 1)
            dve.wait_ge(s_stats, NT)
            for t in range(NT):
                dve.bn_aggr(mv[:, t, :], stats[:, t, :]).then_inc(s_mv, 1)
            dve.wait_ge(s_rstd, 2)
            for t in range(NT):
                dve.tensor_scalar(z[:, t, :], hc[:, t, :], mv[:, t, 0:1], rstd[:, t:t + 1],
                                  ALU.subtract, ALU.mult).then_inc(s_z, 1)

            def pair(a):
                return a[:, :].rearrange("p (t o) -> p t o", o=1).broadcast_to([128, NT, 2])

            dve.wait_ge(s_gate_ps, 1)
            both = ps_gate[:, 0:4 * NT].rearrange("p (t q e) -> p t q e", t=NT, q=2)
            dve.tensor_copy(logits[0:64, :, :], both[0:64, :, 0, :]).then_inc(s_share, 1)
            dve.tensor_copy(logits[64:128, :, :], both[64:128, :, 1, :]).then_inc(s_share, 1)
            dve.wait_ge(s_share, 2)
            dve.tensor_tensor(top[:, :], logits[:, :, 0], logits[:, :, 1], ALU.max).then_inc(s_share, 1)
            dve.wait_ge(s_share, 3)
            dve.tensor_tensor(shifted[:, :, :], logits[:, :, :], pair(top), ALU.subtract).then_inc(s_shift, 1)
            dve.wait_ge(s_exp, 1)
            dve.tensor_tensor(total[:, :], expd[:, :, 0], expd[:, :, 1], ALU.add).then_inc(s_share, 1)
            dve.wait_ge(s_share, 4)
            dve.reciprocal(total_inv[:, :], total[:, :]).then_inc(s_share, 1)
            dve.wait_ge(s_share, 5)
            dve.tensor_tensor(gate[:, :, :], expd[:, :, :], pair(total_inv), ALU.mult).then_inc(s_share, 1)
            dve.wait_ge(s_share, 6)
            dve.tensor_tensor(least[:, :], gate[:, :, 0], gate[:, :, 1], ALU.min).then_inc(s_share, 1)
            dve.wait_ge(s_share, 7)
            dve.tensor_tensor(above[:, :, :], gate[:, :, :], pair(least), ALU.is_gt).then_inc(s_share, 1)
            dve.wait_ge(s_share, 8)
            dve.tensor_tensor(kept[:, :, :], gate[:, :, :], above[:, :, :], ALU.mult).then_inc(s_share, 1)
            dve.wait_ge(s_share, 9)
            dve.tensor_tensor(kept_sum[:, :], kept[:, :, 0], kept[:, :, 1], ALU.add).then_inc(s_share, 1)
            dve.wait_ge(s_share, 10)
            dve.tensor_scalar(kept_clip[:, :], kept_sum[:, :], 1e-6, None, ALU.max).then_inc(s_share, 1)
            dve.wait_ge(s_share, 11)
            dve.reciprocal(kept_inv[:, :], kept_clip[:, :]).then_inc(s_share, 1)
            dve.wait_ge(s_share, 12)
            dve.tensor_tensor(share[:, :, :], kept[:, :, :], pair(kept_inv), ALU.mult).then_inc(s_share, 1)
            dve.wait_ge(s_share, 13)
            for t in range(NT):
                dve.wait_ge(s_y, 2 * t + 2)
                dve.tensor_tensor(y[:, t, :, :], ps_y[t][:, 0:2 * D].rearrange("p (e d) -> p e d", e=2),
                                  b2[:, t, :, :], ALU.add).then_inc(s_yb, 1)
                dve.wait_ge(s_yb, t + 1)
                dve.scalar_tensor_tensor(out=mix[:, t, :], in0=y[:, t, 0, :], scalar=share[:, t, 0:1],
                                         in1=hc[:, t, :], op0=ALU.mult, op1=ALU.add).then_inc(s_mix, 1)
                dve.wait_ge(s_mix, t + 1)
                dve.scalar_tensor_tensor(out=res[:, t, :], in0=y[:, t, 1, :], scalar=share[:, t, 1:2],
                                         in1=mix[:, t, :], op0=ALU.mult, op1=ALU.add).then_inc(s_res, 1)


def vit_layer(nc, dram, out):
    with ExitStack() as ctx:
        h = ctx.enter_context(nc.sbuf_tensor("h", [128, B, 2, D], F32))
        ident = ctx.enter_context(nc.sbuf_tensor("identity", [128, 128], F32))
        w1 = ctx.enter_context(nc.sbuf_tensor("w1", [HF + 1, 2, FF], F32))
        w2 = ctx.enter_context(nc.sbuf_tensor("w2", [128, FC, D], F32))
        b2 = ctx.enter_context(nc.sbuf_tensor("b2", [128, D], F32))
        s_w = ctx.enter_context(nc.semaphore("s_w"))
        phase_one(nc, h, ident, dram, (w1, w2, b2), s_w)
        a1 = ctx.enter_context(nc.sbuf_tensor("a1", [HF + 1, NT, 2, FF], F32))
        gate_w = ctx.enter_context(nc.sbuf_tensor("gate_w", [HF, 2, 2 * NCLS], F32))
        e_b2 = ctx.enter_context(nc.sbuf_tensor("e_b2", [128, NT, 2, D], F32))
        hc = ctx.enter_context(nc.sbuf_tensor("hc", [128, NT, D], F32))
        s_experts = ctx.enter_context(nc.semaphore("s_experts"))
        phase_two(nc, h, ident, dram, out, (w1, w2, b2), s_w, (a1, gate_w, e_b2, hc), s_experts)
        phase_three(nc, ident, dram, out, (a1, gate_w, e_b2, hc), s_experts)


def rope_tables():
    inv = (np.float32(1.0) / np.float32(10000.0) ** (np.arange(0, HD, 2, dtype=np.float32) / np.float32(HD)))
    angle = np.arange(T, dtype=np.float32)[:, None] * inv.astype(np.float32)[None, :]
    cos, sin = np.cos(angle), np.sin(angle)
    return np.concatenate([cos, cos], 1), np.concatenate([-sin, sin], 1)


def by_tiles(rows):
    full = np.zeros((2 * T0, rows.shape[1]), rows.dtype)
    full[:T] = rows
    return np.ascontiguousarray(full.reshape(2, T0, -1).transpose(1, 0, 2))


def in_chunks(w, bias=None):
    full = np.zeros((HF + 1, 2, w.shape[0]), w.dtype)
    full[:HF] = w.T.reshape(2, HF, -1).transpose(1, 0, 2)
    if bias is not None:
        full[HF, 0] = bias
    return full


def kernel(**inputs):
    import concourse.bacc as bacc
    from concourse.bass_utils import run_bass_kernel_spmd

    a = {k: np.asarray(v) for k, v in inputs.items()}
    f32 = np.float32
    patches = a["x"].reshape(B, 3, 14, 16, 14, 16).transpose(0, 1, 3, 5, 2, 4).reshape(B, KC, 128, T - 2)
    x = np.zeros((B, 128, KC, T), f32)
    x[:, :, :, 2:] = patches.transpose(0, 2, 1, 3)
    embed_a = np.concatenate([a["cls_tok"][0], a["L0_tok_cls_token"][0],
                              np.broadcast_to(a["L0_tok_conv_b"], (T - 2, D))])
    embed_b = np.concatenate([np.zeros((1, D), f32), a["L0_tok_pos_emb"][0]])
    cos, sin = rope_tables()
    later = np.where(np.arange(T)[None, :] > np.arange(T)[:, None], f32(FAR), f32(0))
    wq, wk, wv = (a[f"L0_attn_W{n}"] for n in "qkv")
    bqkv = np.concatenate([a[f"L0_attn_b{n}"] for n in "qkv"])
    a1 = np.stack([in_chunks(a["L0_ffn_A1_W"][n].T, a["L0_ffn_A1_b"][n]) for n in range(5)], 1)
    e_b2 = np.zeros((2, 64, NCLS // 2, 2, D), f32)
    for i, e, (_, c) in COMBOS:
        e_b2[i % 2, :, i // 2, e] = a["L0_ffn_A2_b"][c]
    gw = a["L0_ffn_G_W"].transpose(1, 0, 2).reshape(2, HF, 2 * NCLS).transpose(1, 0, 2)
    arrays = {
        "x": x.reshape(B, 128, KC * T),
        "conv_w": a["L0_tok_conv_w"].reshape(D, KC, 128).transpose(2, 1, 0),
        "embed_a": by_tiles(embed_a), "embed_b": by_tiles(embed_b),
        "wqkv": in_chunks(np.concatenate([wq, wk, wv]), bqkv),
        "wo": in_chunks(a["L0_attn_Wo"], a["L0_attn_bo"]),
        "cos": by_tiles(cos), "sin": by_tiles(sin),
        "mask0": later[:T0, :T0], "mask1": later[T0:],
        "ident": np.eye(128, dtype=f32),
        "w1": in_chunks(a["L0_ffn_moe0_W1"].T, a["L0_ffn_moe0_b1"]),
        "w2": a["L0_ffn_moe0_W2"].reshape(FC, 128, D).transpose(1, 0, 2),
        "b2": np.broadcast_to(a["L0_ffn_moe0_b2"], (128, D)),
        "a1": a1, "a2": a["L0_ffn_A2_W"].reshape(5, FC, 128, D).transpose(2, 0, 1, 3),
        "gate_w": gw, "e_b2": e_b2.reshape(128, NCLS // 2, 2, D),
    }
    arrays = {f"in_{k}": np.ascontiguousarray(v) for k, v in arrays.items()}
    nc = bacc.Bacc("TRN2", target_bir_lowering=False, num_devices=1)
    dram = {k[3:]: nc.dram_tensor(k, v.shape, F32, kind="ExternalInput").ap() for k, v in arrays.items()}
    out = nc.dram_tensor("out", [B, T, D], F32, kind="ExternalOutput").ap()
    vit_layer(nc, dram, out)
    result = run_bass_kernel_spmd(nc, [arrays], core_ids=[0])
    return result.results[0]["out"]
```
